# Optimizing a Trainium2 kernel written in Bass

```python
import numpy as np
import jax
import jax.numpy as jnp

def _softmax(x, axis=-1):
    return jax.nn.softmax(x, axis=axis)

def _gelu(x):
    return jax.nn.gelu(x, approximate=True)

def _silu(x):
    return jax.nn.silu(x)

def _sigmoid(x):
    return jax.nn.sigmoid(x)

def _layernorm(x, axis=-1, eps=1e-05):
    m = jnp.mean(x, axis=axis, keepdims=True)
    v = jnp.var(x, axis=axis, keepdims=True)
    return (x - m) / jnp.sqrt(v + eps)

def _scatter_add(tgt, idx, src, axis=0):
    return tgt.at[idx].add(src)

def _segment_sum(src, seg, n):
    return jax.ops.segment_sum(src, seg, n)
kernel_name = 'mk_xattn_ffn_d2_seqx_r8_9b0760'

def setup_inputs(seed: int=0):
    np.random.seed(seed)
    _w = jnp.asarray

    def _rec_inputs():
        import jax
        import jax.numpy as jnp
        _rk = jax.random.key(seed)
        x = -0.0003929 + 0.9999 * jax.random.normal(jax.random.fold_in(_rk, 1), (2, 512, 128), jnp.float32)
        _lenS = 512 - jax.random.randint(jax.random.fold_in(_rk, 7), (2,), 0, max(1, 512 // 4) + 1, jnp.int32)
        _lenS2 = 77 - jax.random.randint(jax.random.fold_in(_rk, 8), (2,), 0, max(1, 77 // 4) + 1, jnp.int32)
        _ctx_1024P = jax.random.normal(jax.random.fold_in(_rk, 11), (2, 16, 128), jnp.float32)
        _ctx_1024c = jax.random.dirichlet(jax.random.fold_in(_rk, 511), 0.3 * jnp.ones((16,), jnp.float32), (2, 77))
        _ctx_1024t = jnp.einsum('bsk,bkd->bsd', _ctx_1024c, _ctx_1024P)
        _ctx_1024t = _ctx_1024t * jax.lax.rsqrt(jnp.mean(jnp.square(_ctx_1024t)) + 1e-12) * 0.953939
        ctx_1024 = 2.81802e-05 + 1.00001 * (_ctx_1024t + 0.3 * jax.random.normal(jax.random.fold_in(_rk, 611), (2, 77, 128), jnp.float32))
        return (x, ctx_1024)
    x, ctx_1024 = _rec_inputs()

    def _L0_xattn_setup():
        import jax, jax.numpy as jnp
        import numpy as np
        DIM = 128
        SCALE_DIM = 4
        QK_DIM = DIM // SCALE_DIM
        B, S = (4, 512)
        key = jax.random.key(seed)
        ks = jax.random.split(key, 8)
        std = 1.0 / np.sqrt(DIM)
        return {'q': jax.random.normal(ks[0], (B, S, DIM), jnp.float32), 'k': jax.random.normal(ks[1], (B, S, DIM), jnp.float32), 'v': jax.random.normal(ks[2], (B, S, DIM), jnp.float32), 'Wq': jax.random.normal(ks[3], (QK_DIM, DIM), jnp.float32) * std, 'bq': jnp.zeros((QK_DIM,), jnp.float32), 'Wk': jax.random.normal(ks[4], (QK_DIM, DIM), jnp.float32) * std, 'bk': jnp.zeros((QK_DIM,), jnp.float32), 'Wv': jax.random.normal(ks[5], (DIM, DIM), jnp.float32) * std, 'bv': jnp.zeros((DIM,), jnp.float32)}
    _L0_xattn_all = _L0_xattn_setup()
    _L0_xattn_in = {k: v for k, v in _L0_xattn_all.items() if k in ('Wq', 'bq', 'Wk', 'bk', 'Wv', 'bv')}
    del _L0_xattn_all

    def _L0_ffn_setup():
        import jax, jax.numpy as jnp
        import numpy as np
        from jax import lax
        D_MODEL = 128
        INTER = 128
        N_EXPERTS = 8
        TOP_K = 2
        ROUTE_SCALE = 1.0
        B, S = (2, 512)
        key = jax.random.key(seed)
        ks = jax.random.split(key, 16)
        sc_d = 1.0 / np.sqrt(D_MODEL)
        sc_f = 1.0 / np.sqrt(INTER)
        inp = {'x': jax.random.normal(ks[0], (B, S, D_MODEL), dtype=jnp.float32), 'gate_w': jax.random.normal(ks[1], (N_EXPERTS, D_MODEL), dtype=jnp.float32) * sc_d, 'w1': jax.random.normal(ks[2], (N_EXPERTS, D_MODEL, INTER), dtype=jnp.float32) * sc_d, 'b1': jnp.zeros((N_EXPERTS, INTER), dtype=jnp.float32), 'w2': jax.random.normal(ks[3], (N_EXPERTS, INTER, D_MODEL), dtype=jnp.float32) * sc_f, 'b2': jnp.zeros((N_EXPERTS, D_MODEL), dtype=jnp.float32), 'w3': jax.random.normal(ks[4], (N_EXPERTS, D_MODEL, INTER), dtype=jnp.float32) * sc_d, 'b3': jnp.zeros((N_EXPERTS, INTER), dtype=jnp.float32), 'sw1': jax.random.normal(ks[5], (D_MODEL, INTER), dtype=jnp.float32) * sc_d, 'sb1': jnp.zeros((INTER,), dtype=jnp.float32), 'sw2': jax.random.normal(ks[6], (INTER, D_MODEL), dtype=jnp.float32) * sc_f, 'sb2': jnp.zeros((D_MODEL,), dtype=jnp.float32), 'sw3': jax.random.normal(ks[7], (D_MODEL, INTER), dtype=jnp.float32) * sc_d, 'sb3': jnp.zeros((INTER,), dtype=jnp.float32)}
        return inp
    _L0_ffn_all = _L0_ffn_setup()
    _L0_ffn_in = {k: v for k, v in _L0_ffn_all.items() if k in ('gate_w', 'w1', 'b1', 'w2', 'b2', 'w3', 'b3', 'sw1', 'sb1', 'sw2', 'sb2', 'sw3', 'sb3')}
    del _L0_ffn_all

    def _L1_xattn_setup():
        import jax, jax.numpy as jnp
        import numpy as np
        import math
        D_MODEL = 128
        N_HEADS = 16
        HEAD_DIM = D_MODEL // N_HEADS
        TOP_K = 32
        SCALE = math.sqrt(HEAD_DIM)

        def _split_heads(t, n):
            B, L, _ = t.shape
            return t.reshape(B, L, N_HEADS, HEAD_DIM).transpose(0, 2, 1, 3)
        key = jax.random.key(seed)
        ks = jax.random.split(key, 12)
        B, S, N = (2, 256, 256)
        std = 1.0 / math.sqrt(D_MODEL)
        inp = {'x': jax.random.normal(ks[0], (B, S, D_MODEL), dtype=jnp.float32), 'knowledge_embeddings': jax.random.normal(ks[1], (B, N, D_MODEL), dtype=jnp.float32), 'Wq': jax.random.normal(ks[2], (D_MODEL, D_MODEL), dtype=jnp.float32) * std, 'bq': jnp.zeros((D_MODEL,), dtype=jnp.float32), 'Wk': jax.random.normal(ks[3], (D_MODEL, D_MODEL), dtype=jnp.float32) * std, 'bk': jnp.zeros((D_MODEL,), dtype=jnp.float32), 'Wv': jax.random.normal(ks[4], (D_MODEL, D_MODEL), dtype=jnp.float32) * std, 'bv': jnp.zeros((D_MODEL,), dtype=jnp.float32), 'Wo': jax.random.normal(ks[5], (D_MODEL, D_MODEL), dtype=jnp.float32) * std, 'bo': jnp.zeros((D_MODEL,), dtype=jnp.float32)}
        return inp
    _L1_xattn_all = _L1_xattn_setup()
    _L1_xattn_in = {k: v for k, v in _L1_xattn_all.items() if k in ('Wq', 'bq', 'Wk', 'bk', 'Wv', 'bv', 'Wo', 'bo')}
    del _L1_xattn_all

    def _L1_ffn_setup():
        import math
        import jax, jax.numpy as jnp
        import numpy as np
        D_MODEL = 128
        D_HIDDEN = 256
        N_EXPERTS = 8
        TOP_K = 2
        CAPACITY_FACTOR = 1.25

        def _moe_forward(x, w_router, w_gate, w_down):
            B, T, D = x.shape
            N = B * T
            xf = x.reshape(N, D)
            logits = xf.astype(jnp.float32) @ w_router.T
            gates = jax.nn.softmax(logits, axis=-1)
            topk_gates, topk_idx = jax.lax.top_k(gates, TOP_K)
            expert_mask = jax.nn.one_hot(topk_idx, N_EXPERTS, dtype=jnp.int32).sum(axis=1)
            capacity = math.ceil(N / N_EXPERTS * CAPACITY_FACTOR)
            position_in_expert = jnp.cumsum(expert_mask, axis=0) - 1
            expert_mask = expert_mask * (position_in_expert < capacity)
            keep = jnp.take_along_axis(expert_mask, topk_idx, axis=1) > 0
            topk_gates = topk_gates * keep
            topk_gates = topk_gates / (topk_gates.sum(axis=-1, keepdims=True) + 1e-06)
            hidden = jax.nn.silu(xf @ w_gate.T)
            combine = (topk_gates[:, :, None] * jax.nn.one_hot(topk_idx, N_EXPERTS, dtype=topk_gates.dtype)).sum(axis=1)
            y = jnp.zeros((N, D), dtype=x.dtype)
            for e in range(N_EXPERTS):
                y = y + combine[:, e:e + 1] * (hidden @ w_down[e].T)
            return y.reshape(B, T, D)
        key = jax.random.key(seed)
        k0, k1, k2, k3 = jax.random.split(key, 4)
        B, T = (2, 256)
        x = jax.random.normal(k0, (B, T, D_MODEL), dtype=jnp.float32)
        w_router = jax.random.normal(k1, (N_EXPERTS, D_MODEL), dtype=jnp.float32) * 0.02
        w_gate = jax.random.normal(k2, (D_HIDDEN, D_MODEL), dtype=jnp.float32) * 0.02
        w_down = jax.random.normal(k3, (N_EXPERTS, D_MODEL, D_HIDDEN), dtype=jnp.float32) * 0.02
        return {'x': x, 'w_router': w_router, 'w_gate': w_gate, 'w_down': w_down}
    _L1_ffn_all = _L1_ffn_setup()
    _L1_ffn_in = {k: v for k, v in _L1_ffn_all.items() if k in ('w_router', 'w_gate', 'w_down')}
    del _L1_ffn_all
    return {'x': x, 'ctx_1024': ctx_1024, 'L0_xattn_Wq': _L0_xattn_in['Wq'], 'L0_xattn_bq': _L0_xattn_in['bq'], 'L0_xattn_Wk': _L0_xattn_in['Wk'], 'L0_xattn_bk': _L0_xattn_in['bk'], 'L0_xattn_Wv': _L0_xattn_in['Wv'], 'L0_xattn_bv': _L0_xattn_in['bv'], 'L0_ffn_gate_w': _L0_ffn_in['gate_w'], 'L0_ffn_w1': _L0_ffn_in['w1'], 'L0_ffn_b1': _L0_ffn_in['b1'], 'L0_ffn_w2': _L0_ffn_in['w2'], 'L0_ffn_b2': _L0_ffn_in['b2'], 'L0_ffn_w3': _L0_ffn_in['w3'], 'L0_ffn_b3': _L0_ffn_in['b3'], 'L0_ffn_sw1': _L0_ffn_in['sw1'], 'L0_ffn_sb1': _L0_ffn_in['sb1'], 'L0_ffn_sw2': _L0_ffn_in['sw2'], 'L0_ffn_sb2': _L0_ffn_in['sb2'], 'L0_ffn_sw3': _L0_ffn_in['sw3'], 'L0_ffn_sb3': _L0_ffn_in['sb3'], 'L1_xattn_Wq': _L1_xattn_in['Wq'], 'L1_xattn_bq': _L1_xattn_in['bq'], 'L1_xattn_Wk': _L1_xattn_in['Wk'], 'L1_xattn_bk': _L1_xattn_in['bk'], 'L1_xattn_Wv': _L1_xattn_in['Wv'], 'L1_xattn_bv': _L1_xattn_in['bv'], 'L1_xattn_Wo': _L1_xattn_in['Wo'], 'L1_xattn_bo': _L1_xattn_in['bo'], 'L1_ffn_w_router': _L1_ffn_in['w_router'], 'L1_ffn_w_gate': _L1_ffn_in['w_gate'], 'L1_ffn_w_down': _L1_ffn_in['w_down']}

def reference(x, ctx_1024, L0_xattn_Wq, L0_xattn_bq, L0_xattn_Wk, L0_xattn_bk, L0_xattn_Wv, L0_xattn_bv, L0_ffn_gate_w, L0_ffn_w1, L0_ffn_b1, L0_ffn_w2, L0_ffn_b2, L0_ffn_w3, L0_ffn_b3, L0_ffn_sw1, L0_ffn_sb1, L0_ffn_sw2, L0_ffn_sb2, L0_ffn_sw3, L0_ffn_sb3, L1_xattn_Wq, L1_xattn_bq, L1_xattn_Wk, L1_xattn_bk, L1_xattn_Wv, L1_xattn_bv, L1_xattn_Wo, L1_xattn_bo, L1_ffn_w_router, L1_ffn_w_gate, L1_ffn_w_down):
    import jax
    import jax.numpy as jnp

    def _L0_xattn_ref(q, k, v, Wq, bq, Wk, bk, Wv, bv):
        import jax, jax.numpy as jnp
        import numpy as np
        DIM = 128
        SCALE_DIM = 4
        QK_DIM = DIM // SCALE_DIM
        B, S = (4, 512)
        scale = jnp.asarray(np.sqrt(QK_DIM), q.dtype)
        qp = jnp.einsum('bsd,ed->bse', q, Wq) + bq
        kp = jnp.einsum('bsd,ed->bse', k, Wk) + bk
        vp = jnp.einsum('bsd,ed->bse', v, Wv) + bv
        z = jnp.einsum('bqe,bke->bqk', qp, kp)
        z = jax.nn.sigmoid(z / scale)
        return jnp.einsum('bqk,bkd->bqd', z, vp)

    def _L0_ffn_ref(x, gate_w, w1, b1, w2, b2, w3, b3, sw1, sb1, sw2, sb2, sw3, sb3):
        import jax, jax.numpy as jnp
        import numpy as np
        from jax import lax
        D_MODEL = 128
        INTER = 128
        N_EXPERTS = 8
        TOP_K = 2
        ROUTE_SCALE = 1.0
        B, S = (2, 512)
        Bx, Sx, D = x.shape
        xt = x.reshape(-1, D)
        scores = jax.nn.softmax((xt @ gate_w.T).astype(jnp.float32), axis=-1)
        top_vals, top_idx = lax.top_k(scores, TOP_K)
        weights = (top_vals * ROUTE_SCALE).astype(x.dtype)
        combine = jnp.sum(jax.nn.one_hot(top_idx, N_EXPERTS, dtype=x.dtype) * weights[..., None], axis=1)

        def body(acc, p):
            W1, B1, W2, B2, W3, B3, c = p
            h = jax.nn.silu(xt @ W1 + B1) * (xt @ W3 + B3)
            return (acc + c[:, None] * (h @ W2 + B2), None)
        y, _ = lax.scan(body, jnp.zeros_like(xt), (w1, b1, w2, b2, w3, b3, combine.T))
        z = jax.nn.silu(xt @ sw1 + sb1) * (xt @ sw3 + sb3) @ sw2 + sb2
        return (y + z).reshape(Bx, Sx, D)

    def _L1_xattn_ref(x, knowledge_embeddings, Wq, bq, Wk, bk, Wv, bv, Wo, bo):
        import jax, jax.numpy as jnp
        import numpy as np
        import math
        D_MODEL = 128
        N_HEADS = 16
        HEAD_DIM = D_MODEL // N_HEADS
        TOP_K = 32
        SCALE = math.sqrt(HEAD_DIM)

        def _split_heads(t, n):
            B, L, _ = t.shape
            return t.reshape(B, L, N_HEADS, HEAD_DIM).transpose(0, 2, 1, 3)
        B, S, _ = x.shape
        N = knowledge_embeddings.shape[1]
        Q = _split_heads(x @ Wq.T + bq, N_HEADS)
        K = _split_heads(knowledge_embeddings @ Wk.T + bk, N_HEADS)
        V = _split_heads(knowledge_embeddings @ Wv.T + bv, N_HEADS)
        scores = jnp.einsum('bhsd,bhnd->bhsn', Q, K) / SCALE
        k = min(TOP_K, N)
        topk_scores, topk_indices = jax.lax.top_k(scores, k)
        sparse_weights = jax.nn.softmax(topk_scores, axis=-1)
        sel_V = jnp.take_along_axis(V[:, :, None, :, :], topk_indices[..., None], axis=3)
        context = jnp.einsum('bhsk,bhskd->bhsd', sparse_weights, sel_V)
        context = context.transpose(0, 2, 1, 3).reshape(B, S, D_MODEL)
        return context @ Wo.T + bo

    def _L1_ffn_ref(x, w_router, w_gate, w_down):
        import math
        import jax, jax.numpy as jnp
        import numpy as np
        D_MODEL = 128
        D_HIDDEN = 256
        N_EXPERTS = 8
        TOP_K = 2
        CAPACITY_FACTOR = 1.25

        def _moe_forward(x, w_router, w_gate, w_down):
            B, T, D = x.shape
            N = B * T
            xf = x.reshape(N, D)
            logits = xf.astype(jnp.float32) @ w_router.T
            gates = jax.nn.softmax(logits, axis=-1)
            topk_gates, topk_idx = jax.lax.top_k(gates, TOP_K)
            expert_mask = jax.nn.one_hot(topk_idx, N_EXPERTS, dtype=jnp.int32).sum(axis=1)
            capacity = math.ceil(N / N_EXPERTS * CAPACITY_FACTOR)
            position_in_expert = jnp.cumsum(expert_mask, axis=0) - 1
            expert_mask = expert_mask * (position_in_expert < capacity)
            keep = jnp.take_along_axis(expert_mask, topk_idx, axis=1) > 0
            topk_gates = topk_gates * keep
            topk_gates = topk_gates / (topk_gates.sum(axis=-1, keepdims=True) + 1e-06)
            hidden = jax.nn.silu(xf @ w_gate.T)
            combine = (topk_gates[:, :, None] * jax.nn.one_hot(topk_idx, N_EXPERTS, dtype=topk_gates.dtype)).sum(axis=1)
            y = jnp.zeros((N, D), dtype=x.dtype)
            for e in range(N_EXPERTS):
                y = y + combine[:, e:e + 1] * (hidden @ w_down[e].T)
            return y.reshape(B, T, D)
        return _moe_forward(x, w_router, w_gate, w_down)
    x = x + _L0_xattn_ref(_layernorm(x, axis=-1), ctx_1024, ctx_1024, L0_xattn_Wq, L0_xattn_bq, L0_xattn_Wk, L0_xattn_bk, L0_xattn_Wv, L0_xattn_bv)
    x = x + _L0_ffn_ref(_layernorm(x, axis=-1), L0_ffn_gate_w, L0_ffn_w1, L0_ffn_b1, L0_ffn_w2, L0_ffn_b2, L0_ffn_w3, L0_ffn_b3, L0_ffn_sw1, L0_ffn_sb1, L0_ffn_sw2, L0_ffn_sb2, L0_ffn_sw3, L0_ffn_sb3)
    x = x + _L1_xattn_ref(_layernorm(x, axis=-1), ctx_1024, L1_xattn_Wq, L1_xattn_bq, L1_xattn_Wk, L1_xattn_bk, L1_xattn_Wv, L1_xattn_bv, L1_xattn_Wo, L1_xattn_bo)
    x = x + _L1_ffn_ref(_layernorm(x, axis=-1), L1_ffn_w_router, L1_ffn_w_gate, L1_ffn_w_down)
    return x

_drawn_inputs = setup_inputs


def setup_inputs(seed=0):
    import zlib

    import numpy as np

    out = dict(_drawn_inputs(seed))
    spreads = {'L0_xattn_bq': (0.0, 0.294),
     'L0_xattn_bk': (0.0, 0.429),
     'L0_xattn_bv': (0.0, 0.1),
     'L0_ffn_b1': (0.0, 0.8),
     'L0_ffn_b2': (0.0, 2.0),
     'L0_ffn_b3': (0.0, 0.8),
     'L0_ffn_sb1': (0.0, 2.0),
     'L0_ffn_sb2': (0.0, 2.0),
     'L0_ffn_sb3': (0.0, 2.0),
     'L1_xattn_bq': (0.0, 2.0),
     'L1_xattn_bk': (0.0, 2.0),
     'L1_xattn_bv': (0.0, 2.0),
     'L1_xattn_bo': (0.0, 2.0)}
    factors = {'L0_ffn_gate_w': 4.333,
     'L0_ffn_w1': 4.853,
     'L0_ffn_w2': 4.412,
     'L0_ffn_w3': 4.734,
     'L1_xattn_Wq': 13.657,
     'L1_xattn_Wk': 10.344,
     'L1_ffn_w_router': 8.0,
     'L1_ffn_w_gate': 25.174,
     'L1_ffn_w_down': 22.33,
     'L0_ffn_sw1': 4.097,
     'L0_ffn_sw2': 3.472,
     'L0_ffn_sw3': 3.55,
     'L1_xattn_Wv': 3.264,
     'L1_xattn_Wo': 2.735}
    for name, (base, spread) in spreads.items():
        noise = np.random.default_rng([zlib.crc32(name.encode()), seed]).standard_normal(out[name].shape)
        drawn = base * np.exp(spread * noise) if base else spread * noise
        out[name] = jnp.asarray(drawn.astype(out[name].dtype))
    for name, factor in factors.items():
        out[name] = (out[name] * factor).astype(out[name].dtype)
    return out
```

```python
from contextlib import ExitStack

import concourse.bass as bass
from concourse import mybir

F32 = mybir.dt.float32
BF16 = mybir.dt.bfloat16
U32 = mybir.dt.uint32
ALU = mybir.AluOpType
ACT = mybir.ActivationFunctionType

B, S, D = 2, 512, 128
KEYS = 77
P = 128
TILES = B * S // P
PER_BATCH = S // P
QK = 32
E = 8
INTER = 128
HIDDEN = 256
HEADS, HD = 16, 8
TOPK = 32
GROUPS = 4
HG = HEADS // GROUPS
GK = HG * KEYS
CAPACITY = float(-(-(B * S * 5) // (E * 4)))
EPS = 1e-5
TAKEN = -3.0e38

EARLY = [("ident", 128), ("ctxT", B * KEYS), ("wk0", QK), ("wq0", 2 * QK), ("wv0", D), ("bq0", 1), ("bk0", 1),
         ("sel", TILES), ("iota", E), ("gate", E)]
LATE = [("wq1", D), ("wk1", D), ("wv1", D), ("wo1", D), ("router", E), ("wg", HIDDEN), ("triu", P), ("ones", P),
        ("headmask", HEADS), ("bq1", 1), ("bk1", 1), ("bias", 18)]
NBIAS = 2 * E * INTER + 2 * INTER


def columns(fields):
    at, where = 0, {}
    for name, width in fields:
        where[name] = (at, at + width)
        at += width
    return where, at


EARLY_AT, EARLY_W = columns(EARLY)
LATE_AT, LATE_W = columns(LATE)


def build(nc, early_d, late_d, x_d, rows_d, w1_d, w3_d, w2_d, sw13_d, sw2_d, b2_d, wd_d, out_d):
    ctx = ExitStack()
    with ctx:
        def sb(name, shape, dt=F32):
            return ctx.enter_context(nc.sbuf_tensor(name, shape, dt))

        def psum(name, cols=512):
            return ctx.enter_context(nc.psum_tensor(name, [128, cols], F32))

        def sem(name):
            return ctx.enter_context(nc.semaphore(name))

        early = sb("early", [128, EARLY_W])
        late = sb("late", [128, LATE_W])

        def e(name):
            a, b = EARLY_AT[name]
            return early[:, a:b]

        def l(name):
            a, b = LATE_AT[name]
            return late[:, a:b]

        ident, ctxT = e("ident"), e("ctxT")
        rows = sb("rows", [128, 3 * D])
        bv0, bv1, bo = rows[:, 0:D], rows[:, D:2 * D], rows[:, 2 * D:3 * D]
        w1 = sb("w1", [D, E * INTER])
        w3 = sb("w3", [D, E * INTER])
        w2 = sb("w2", [INTER, E * D])
        sw13 = sb("shared_w13", [D, 2 * INTER])
        sw2 = sb("shared_w2", [INTER, D])
        b2 = sb("b2", [E + 1, D])
        wd = sb("wd", [128, 2, E * D])
        bias_dram = nc.dram_tensor("bias_parts", [3, NBIAS], BF16, kind="Internal").ap()
        bias_hml = sb("bias_hml", [128, 3, 18], BF16)
        bias_rest = sb("bias_rest", [128, 2, 18])
        bias3 = sb("bias3", [3, NBIAS], BF16)
        ones3 = sb("ones3", [3, P], BF16)
        eps_t = sb("eps_t", [128, 1])
        half_t = sb("half_t", [128, 1])

        k0 = sb("k0", [2 * QK, KEYS])
        v0 = sb("v0", [KEYS, B, D])
        qsel_bias = sb("qsel_bias", [2 * QK, TILES])
        k1 = sb("k1", [D, B, KEYS])
        kbd = sb("kbd", [D, B, HEADS, KEYS])
        v1 = sb("v1", [KEYS, B, HEADS, HD + 1])

        x = sb("x", [P, TILES, D])
        lnst = [sb(f"lnst{k}", [P, 6]) for k in range(4)]
        lnmv = [sb(f"lnmv{k}", [P, 2]) for k in range(4)]
        lnve = [sb(f"lnve{k}", [P, 1]) for k in range(4)]
        lnrs = [sb(f"lnrs{k}", [P, 1]) for k in range(4)]
        xn = [sb(f"xn{k}", [P, D]) for k in range(4)]
        xT = [sb(f"xT{k}", [D, P]) for k in range(4)]
        q0 = sb("q0", [2 * QK, P])
        th0 = sb("th0", [KEYS, P])
        sg0 = sb("sg0", [KEYS, P])
        gmax = [sb(f"gmax{k}", [P, 8]) for k in range(2)]
        gidx = [sb(f"gidx{k}", [P, 8], U32) for k in range(2)]
        gidf = [sb(f"gidf{k}", [P, 2]) for k in range(2)]
        glog = [sb(f"glog{k}", [P, E]) for k in range(2)]
        gexp = [sb(f"gexp{k}", [P, E]) for k in range(2)]
        gsum = [sb(f"gsum{k}", [P, 1]) for k in range(2)]
        grec = [sb(f"grec{k}", [P, 1]) for k in range(2)]
        gone = [sb(f"gone{k}", [P, 2, E]) for k in range(2)]
        gmask = [sb(f"gmask{k}", [P, E]) for k in range(2)]
        c0 = sb("c0", [P, E + 1])
        c0T = sb("c0T", [E + 1, P])
        act0 = sb("act0", [P, E + 1, INTER])
        lin0 = sb("lin0", [P, E + 1, INTER])
        g0 = sb("g0", [P, E + 1, INTER])
        g0T = sb("g0T", [INTER, E + 1, P])
        qT1 = sb("qT1", [D, P])
        sw = [sb(f"scores{g}", [P, 2, GK]) for g in range(GROUPS)]
        top1 = sb("top1", [P, HEADS, 8])
        topr = sb("topr", [P, HEADS, 8])
        peak = sb("peak", [P, HEADS])
        ex = sb("ex", [P, 2, GK])
        pw = sb("pw", [P, GK])
        pT = [sb(f"pT{n}", [KEYS, HG * P]) for n in range(2)]
        rden = sb("rden", [P, HEADS])
        cx = sb("cx", [P, HEADS, HD])
        cxT = sb("cxT", [D, P])
        kept_before = sb("kept_before", [P, E])
        keep = sb("keep", [P, E])
        tg = sb("tg", [P, E])
        tgs = sb("tgs", [P, 1])
        tge = sb("tge", [P, 1])
        tgr = sb("tgr", [P, 1])
        c1 = sb("c1", [P, E])
        hid = sb("hid", [P, HIDDEN])
        hidT = sb("hidT", [128, 2, P])
        y1 = sb("y1", [P, E * D])
        y1c = sb("y1c", [P, E * D])
        s4 = sb("s4", [P, 4 * D])
        s2 = sb("s2", [P, 2 * D])
        s1 = sb("s1", [P, D])
        xo = sb("xo", [P, D])

        pA = psum("pA")
        pB = psum("pB")
        pD = psum("pD")
        pO = psum("pO")
        R0 = psum("R0")
        R1 = psum("R1")
        W = [psum("W0"), psum("W1")]
        pv_out = pO[:, 0:HEADS * (HD + 1)].rearrange("p (h d) -> p h d", h=HEADS)
        logits = [pB[:, 384:392], pD[:, 384:392]]
        c0T_ps = pB[0:E + 1, 0:128]
        count_ps = pD[:, 392:400]
        xT_ps = [pA[:, 0:128], pB[:, 0:128], pB[:, 256:384], pD[:, 256:384]]

        early_in, late_in, x0_in, x_in, rows_in = (sem(n) for n in ("early_in", "late_in", "x0_in", "x_in", "rows_in"))
        w13_in, w2_in, wd_in, bias_out, bias_in = (sem(n) for n in ("w13_in", "w2_in", "wd_in", "bias_out", "bias_in"))
        stored = sem("stored")
        passed = sem("passed")
        consts_set, bias_split, kv_mm, kv_act, kv_dve, kv_pool = (
            sem(n) for n in ("consts_set", "bias_split", "kv_mm", "kv_act", "kv_dve", "kv_pool"))
        ln_stats = [sem(f"ln_stats{k}") for k in range(4)]
        ln_mv = [sem(f"ln_mv{k}") for k in range(4)]
        ln_ve = [sem(f"ln_ve{k}") for k in range(4)]
        ln_rstd = [sem(f"ln_rstd{k}") for k in range(4)]
        ln_done = [sem(f"ln_done{k}") for k in range(4)]
        xT_mm = [sem(f"xT_mm{k}") for k in range(4)]
        xT_in = [sem(f"xT_in{k}") for k in range(4)]
        q0_mm, q0_act, z0_mm, tanh0, sigm0, o0_mm, x_attn0 = (
            sem(n) for n in ("q0_mm", "q0_act", "z0_mm", "tanh0", "sigm0", "o0_mm", "x_attn0"))
        rt_mm, rt_max, rt_idx, rt_log, rt_exp, rt_rec, rt_idf, rt_one, rt_mask = (
            [sem(f"{n}{k}") for k in range(2)] for n in
            ("rt_mm", "rt_max", "rt_idx", "rt_log", "rt_exp", "rt_rec", "rt_idf", "rt_one", "rt_mask"))
        c0_part, c0_set, c0T_mm, c0T_act = (sem(n) for n in ("c0_part", "c0_set", "c0T_mm", "c0T_act"))
        h1_mm, h3_mm, h1_act, h3_act, g0_lin, g0_set, g0T_mm, g0T_act = (
            sem(n) for n in ("h1_mm", "h3_mm", "h1_act", "h3_act", "g0_lin", "g0_set", "g0T_mm", "g0T_act"))
        y0_mm, x_moe0, x_bo = (sem(n) for n in ("y0_mm", "x_moe0", "x_bo"))
        q1_mm, q1_act, s1_mm, s1_act = (sem(n) for n in ("q1_mm", "q1_act", "s1_mm", "s1_act"))
        step, best_found = sem("step"), sem("best_found")
        less_max, exps, weights_set, pT_mm, pT_act, pv_mm = (
            sem(n) for n in ("less_max", "exps", "weights_set", "pT_mm", "pT_act", "pv_mm"))
        den_rec, cx_set, cxT_mm, cxT_act, o1_mm, x_attn1 = (
            sem(n) for n in ("den_rec", "cx_set", "cxT_mm", "cxT_act", "o1_mm", "x_attn1"))
        hid_mm, hid_act, hidT_mm, hidT_act, cnt_mm, kept_add = (
            sem(n) for n in ("hid_mm", "hid_act", "hidT_mm", "hidT_act", "cnt_mm", "kept_add"))
        keep_set, tg_set, tge_set, tgr_set, c1_set = (
            sem(n) for n in ("keep_set", "tg_set", "tge_set", "tgr_set", "c1_set"))
        y1_mm, y1_act, y1_mul, y1_s4, y1_s2, y1_s1, xo_set = (
            sem(n) for n in ("y1_mm", "y1_act", "y1_mul", "y1_s4", "y1_s2", "y1_s1", "xo_set"))

        FIRST, LAST = 2, TILES - 3

        def real(t):
            return not isinstance(t, int) or 0 <= t < TILES

        def pass_when(eng, s, value):
            eng.wait_ge(s, value)
            if not isinstance(value, int):
                eng.sem_inc(passed)

        def iterations(eng, body):
            for i in range(-2, FIRST):
                body(i)
            with eng.Fori(FIRST, LAST + 1) as i:
                body(i)
            for i in range(LAST + 1, TILES + 2):
                body(i)

        block = ctx.enter_context(nc.Block())

        @block.sync
        def _(sp):
            sp.dma_start(early[:], early_d).then_inc(early_in, 16)
            sp.dma_start(x[:, 0, :], x_d[0]).then_inc(x0_in, 16)
            sp.dma_start(rows[:], rows_d.partition_broadcast(128)).then_inc(rows_in, 16)
            sp.dma_start(late[:], late_d).then_inc(late_in, 16)
            sp.dma_start(w1[:], w1_d).then_inc(w13_in, 16)
            sp.dma_start(w3[:], w3_d).then_inc(w13_in, 16)
            sp.dma_start(sw13[:], sw13_d).then_inc(w13_in, 16)
            sp.dma_start(x[:, 1:, :], x_d[1:].rearrange("t p d -> p t d")).then_inc(x_in, 16)
            sp.wait_ge(bias_split, 5)
            sp.dma_start(bias_dram.rearrange("k (p j) -> p k j", j=18), bias_hml[:]).then_inc(bias_out, 16)
            sp.wait_ge(bias_out, 16)
            sp.dma_start(bias3[:], bias_dram).then_inc(bias_in, 16)
            sp.dma_start(w2[:], w2_d).then_inc(w2_in, 16)
            sp.dma_start(sw2[:], sw2_d).then_inc(w2_in, 16)
            sp.dma_start(b2[:], b2_d).then_inc(w2_in, 16)
            sp.dma_start(wd[:], wd_d).then_inc(wd_in, 16)

            def store(t):
                pass_when(sp, xo_set, t + 1)
                sp.dma_start(out_d[t], xo[:]).then_inc(stored, 16)

            def body(i):
                if real(i - 2):
                    store(i - 2)
            iterations(sp, body)
            sp.wait_ge(stored, 16 * (TILES + 1))

        @block.tensor
        def _(pe):
            pe.wait_ge(early_in, 16)
            for b in range(B):
                cb = ctxT[:, b * KEYS:(b + 1) * KEYS]
                nc.tensor.matmul(R0[b * QK:(b + 1) * QK, 0:KEYS], e("wk0"), cb, start=True, stop=True)
                last = nc.tensor.matmul(R1[0:KEYS, b * D:(b + 1) * D], cb, e("wv0"), start=True, stop=True)
            last.then_inc(kv_mm, 1)

            def later_keys():
                pe.wait_ge(late_in, 16)
                nc.tensor.matmul(W[0][:, 0:B * KEYS], l("wk1"), ctxT, start=True, stop=True)
                for b in range(B):
                    last = nc.tensor.matmul(W[1][0:KEYS, b * D:(b + 1) * D], ctxT[:, b * KEYS:(b + 1) * KEYS],
                                            l("wv1"), start=True, stop=True)
                last.then_inc(kv_mm, 1)

            def turn_xn(k, t):
                pe.wait_ge(ln_done[k], t + 1)
                nc.tensor.transpose(xT_ps[k], xn[k][:], ident).then_inc(xT_mm[k], 1)

            def attn0_q(t):
                pe.wait_ge(xT_in[0], t + 1)
                nc.tensor.matmul(pA[0:2 * QK, 128:256], e("wq0"), xT[0][:], start=True, stop=True).then_inc(q0_mm, 1)

            def attn0_z(t):
                pe.wait_ge(q0_act, t + 1)
                if isinstance(t, int):
                    pe.wait_ge(kv_act, 2)
                nc.tensor.matmul(pA[0:KEYS, 256:384], k0[:], q0[:], start=True, stop=True).then_inc(z0_mm, 1)

            def attn0_o(t):
                if isinstance(t, int):
                    pe.wait_ge(kv_dve, 1)
                pe.wait_ge(sigm0, t + 1)
                nc.tensor.matmul(pA[:, 384:512], sg0[:], v0[:, t // PER_BATCH, :],
                                 start=True, stop=True).then_inc(o0_mm, 1)

            def route(k, t):
                pe.wait_ge(xT_in[k * 2 + 1], t + 1)
                nc.tensor.matmul(logits[k], xT[k * 2 + 1][:], e("gate") if k == 0 else l("router"),
                                 start=True, stop=True).then_inc(rt_mm[k], 1)

            def experts(j, t):
                if isinstance(t, int):
                    pe.wait_ge(w13_in, 48)
                    pe.wait_ge(bias_in, 16)
                    pe.wait_ge(consts_set, 5)
                cols = slice(j * 512, (j + 1) * 512)
                if j == 1:
                    pe.wait_ge(h1_act, 3 * t + 1)
                elif isinstance(t, int) and t == 0:
                    pe.wait_ge(kv_act, 2)
                else:
                    pe.wait_ge(s1_act, GROUPS * t - 1)
                nc.tensor.matmul(R0[:], ones3[:], bias3[:, cols], start=True, stop=False)
                nc.tensor.matmul(R0[:], xT[1][:], w1[:, cols], start=False, stop=True).then_inc(h1_mm, 1)
                if j == 1:
                    pe.wait_ge(h3_act, 3 * t + 1)
                elif isinstance(t, int) and t == 0:
                    pe.wait_ge(kv_dve, 1)
                else:
                    pe.wait_ge(s1_act, GROUPS * t)
                nc.tensor.matmul(R1[:], ones3[:], bias3[:, E * INTER + j * 512:E * INTER + (j + 1) * 512],
                                 start=True, stop=False)
                nc.tensor.matmul(R1[:], xT[1][:], w3[:, cols], start=False, stop=True).then_inc(h3_mm, 1)

            def shared(t):
                pe.wait_ge(h1_act, 3 * t + 2)
                nc.tensor.matmul(R0[:, 0:256], ones3[:], bias3[:, 2 * E * INTER:], start=True, stop=False)
                nc.tensor.matmul(R0[:, 0:256], xT[1][:], sw13[:], start=False, stop=True).then_inc(h1_mm, 1)

            def hidden(t):
                if not real(t + 3):
                    pe.wait_ge(y1_act, 2 * t)
                nc.tensor.matmul(R0[:, 256:512], xT[3][:], l("wg"), start=True, stop=True).then_inc(hid_mm, 1)

            def turn_c0(t):
                pe.wait_ge(c0_set, t + 1)
                nc.tensor.transpose(c0T_ps, c0[:], ident).then_inc(c0T_mm, 1)

            def turn_g(j, t):
                bank = (R1, R0, R1)[j]
                pe.wait_ge(g0_set, 3 * t + j + 1)
                if j == 0:
                    pe.wait_ge(h3_act, 3 * t + 2)
                elif j == 1:
                    pe.wait_ge(h3_act, 3 * t + 3)
                    pe.wait_ge(h1_act, 3 * t + 3)
                    if real(t - 3):
                        pe.wait_ge(hid_act, t - 2)
                else:
                    pe.wait_ge(g0T_act, 3 * t + 1)
                for n in range(4 if j < 2 else 1):
                    last = nc.tensor.transpose(bank[:, n * 128:(n + 1) * 128], g0[:, 4 * j + n, :], ident)
                last.then_inc(g0T_mm, 1)

            def turn_hidden(t):
                pe.wait_ge(hid_act, t + 1)
                if not real(t + 3):
                    pe.wait_ge(y1_act, 2 * t)
                for n in range(2):
                    last = nc.tensor.transpose(R1[:, 256 + n * 128:384 + n * 128], hid[:, n * 128:(n + 1) * 128],
                                               ident)
                last.then_inc(hidT_mm, 1)

            def moe0_out(t):
                if isinstance(t, int):
                    pe.wait_ge(w2_in, 48)
                pe.wait_ge(c0T_act, t + 1)
                nc.tensor.matmul(pB[:, 128:256], c0T[:], b2[:], start=True, stop=False)
                for j in range(3):
                    pe.wait_ge(g0T_act, 3 * t + j + 1)
                    for n in range(4 if j < 2 else 1):
                        w = w2[:, (4 * j + n) * D:(4 * j + n + 1) * D] if j < 2 else sw2[:]
                        last = nc.tensor.matmul(pB[:, 128:256], g0T[:, 4 * j + n, :], w, start=False, stop=(j == 2))
                last.then_inc(y0_mm, 1)

            def counts(t):
                pe.wait_ge(rt_log[1], t + 1)
                pe.wait_ge(rt_mask[1], t + 1)
                nc.tensor.matmul(count_ps, l("triu"), gmask[1][:], start=True, stop=False)
                pe.wait_ge(kept_add, t + 1)
                nc.tensor.matmul(count_ps, l("ones"), kept_before[:], start=False, stop=True).then_inc(cnt_mm, 1)

            def moe1_out(n, t):
                pe.wait_ge(wd_in, 16)
                pe.wait_ge(hidT_act, t + 1)
                if real(t + 3):
                    pe.wait_ge(g0T_act, 3 * (t + 3) + 3)
                for k in range(2):
                    last = nc.tensor.matmul((R0, R1)[n][:], hidT[:, k, :], wd[:, k, n * 512:(n + 1) * 512],
                                            start=(k == 0), stop=(k == 1))
                last.then_inc(y1_mm, 1)

            def queries1(t):
                pe.wait_ge(xT_in[2], t + 1)
                nc.tensor.matmul(pB[:, 384:512], l("wq1"), xT[2][:], start=True, stop=True).then_inc(q1_mm, 1)

            def scores(g, t):
                bank = (R0, R1)[g % 2]
                if isinstance(t, int):
                    pe.wait_ge(kv_pool, 2)
                if g == 0:
                    pe.wait_ge(q1_act, t + 1)
                if g < 2:
                    if real(t - 3):
                        pe.wait_ge(y1_act, 2 * (t - 3) + g + 1)
                    pe.wait_ge(g0T_act, 3 * t + 3)
                else:
                    pe.wait_ge(s1_act, GROUPS * t + g - 1)
                nc.tensor.matmul(bank[:, 0:GK], qT1[:],
                                 kbd[:, t // PER_BATCH, g * HG:(g + 1) * HG, :].rearrange("p h k -> p (h k)"),
                                 start=True, stop=True).then_inc(s1_mm, 1)

            def turn_weights(g, t):
                n = GROUPS * t + g
                pe.wait_ge(weights_set, n + 1)
                if not (isinstance(t, int) and n < 2):
                    pe.wait_ge(pT_act, n - 1)
                for h in range(HG):
                    last = nc.tensor.transpose(W[g % 2][0:KEYS, h * P:(h + 1) * P], pw[:, h * KEYS:(h + 1) * KEYS],
                                               ident)
                last.then_inc(pT_mm, 1)

            def weigh_values(g, t):
                if isinstance(t, int):
                    pe.wait_ge(kv_dve, 3)
                if g == 0 and real(t - 1):
                    pe.wait_ge(cx_set, t)
                pe.wait_ge(pT_act, GROUPS * t + g + 1)
                for h in range(HG):
                    last = nc.tensor.matmul(pv_out[:, g * HG + h, :], pT[g % 2][:, h * P:(h + 1) * P],
                                            v1[:, t // PER_BATCH, g * HG + h, :], start=True, stop=True)
                last.then_inc(pv_mm, 1)

            def turn_cx(t):
                if not (isinstance(t, int) and t == 0):
                    pe.wait_ge(keep_set, t)
                pe.wait_ge(cx_set, t + 1)
                nc.tensor.transpose(pD[:, 0:128], cx[:].rearrange("p h d -> p (h d)"), ident).then_inc(cxT_mm, 1)

            def project1(t):
                pe.wait_ge(cxT_act, t + 1)
                nc.tensor.matmul(pD[:, 128:256], cxT[:], l("wo1"), start=True, stop=True).then_inc(o1_mm, 1)

            def body(i):
                a, b, c, d, m = i + 2, i + 1, i, i - 1, i - 2
                if isinstance(i, int) and i == -1:
                    later_keys()
                if real(c):
                    scores(3, c)
                if real(b):
                    experts(0, b)
                if real(d):
                    turn_weights(3, d)
                if real(b):
                    experts(1, b)
                if real(d):
                    weigh_values(3, d)
                if real(b):
                    shared(b)
                if real(m):
                    hidden(m)
                if real(b):
                    turn_c0(b)
                if real(d):
                    turn_cx(d)
                if real(b):
                    turn_g(0, b)
                if real(d):
                    project1(d)
                if real(b):
                    turn_g(1, b)
                    turn_g(2, b)
                if real(m):
                    turn_hidden(m)
                if real(c):
                    turn_weights(0, c)
                if real(b):
                    moe0_out(b)
                if real(c):
                    weigh_values(0, c)
                if real(a):
                    turn_xn(0, a)
                    attn0_q(a)
                if real(d):
                    turn_xn(3, d)
                if real(m):
                    moe1_out(0, m)
                if real(a):
                    attn0_z(a)
                if real(d):
                    route(1, d)
                if real(m):
                    moe1_out(1, m)
                if real(c):
                    turn_weights(1, c)
                if real(a):
                    attn0_o(a)
                if real(c):
                    weigh_values(1, c)
                if real(b):
                    turn_xn(2, b)
                    queries1(b)
                if real(d):
                    counts(d)
                if real(b):
                    scores(0, b)
                if real(a):
                    turn_xn(1, a)
                if real(c):
                    turn_weights(2, c)
                if real(b):
                    scores(1, b)
                if real(a):
                    route(0, a)
                if real(c):
                    weigh_values(2, c)
                if real(b):
                    scores(2, b)
            iterations(pe, body)

        @block.vector
        def _(dve):
            nc.vector.memset(eps_t[:], EPS).then_inc(consts_set, 1)
            nc.vector.memset(half_t[:], -0.5).then_inc(consts_set, 1)
            nc.vector.memset(ones3[:], 1.0).then_inc(consts_set, 1)
            nc.vector.memset(c0[:, E:E + 1], 1.0).then_inc(consts_set, 1)
            nc.vector.memset(v1[:, :, :, HD:HD + 1], 1.0).then_inc(consts_set, 1)

            def values0():
                dve.wait_ge(kv_mm, 1)
                dve.wait_ge(rows_in, 16)
                nc.vector.tensor_tensor(v0[:], R1[0:KEYS, 0:B * D].rearrange("p (b d) -> p b d", b=B),
                                        bv0[0:KEYS].unsqueeze(1).to_broadcast([KEYS, B, D]),
                                        ALU.add).then_inc(kv_dve, 1)

            def split_bias():
                dve.wait_ge(late_in, 16)
                nc.vector.tensor_copy(bias_hml[:, 0], l("bias")).then_inc(bias_split, 1)
                dve.wait_ge(bias_split, 1)
                nc.vector.tensor_tensor(bias_rest[:, 0], l("bias"), bias_hml[:, 0], ALU.subtract).then_inc(bias_split, 1)
                dve.wait_ge(bias_split, 2)
                nc.vector.tensor_copy(bias_hml[:, 1], bias_rest[:, 0]).then_inc(bias_split, 1)
                dve.wait_ge(bias_split, 3)
                nc.vector.tensor_tensor(bias_rest[:, 1], bias_rest[:, 0], bias_hml[:, 1],
                                        ALU.subtract).then_inc(bias_split, 1)
                dve.wait_ge(bias_split, 4)
                nc.vector.tensor_copy(bias_hml[:, 2], bias_rest[:, 1]).then_inc(bias_split, 1)

            def values1():
                dve.wait_ge(kv_mm, 2)
                for b in range(B):
                    nc.vector.tensor_tensor(v1[:, b, :, 0:HD],
                                            W[1][0:KEYS, b * D:(b + 1) * D].rearrange("p (h d) -> p h d", h=HEADS),
                                            bv1[0:KEYS].rearrange("p (h d) -> p h d", h=HEADS),
                                            ALU.add).then_inc(kv_dve, 1)

            def stats(k, t):
                if k == 0:
                    if isinstance(t, int):
                        dve.wait_ge(x0_in if t == 0 else x_in, 16)
                else:
                    pass_when(dve, (x_attn0, x_moe0, x_attn1)[k - 1], t + 1)
                nc.vector.bn_stats(lnst[k][:], x[:, t, :]).then_inc(ln_stats[k], 1)
                pass_when(dve, ln_stats[k], t + 1)
                nc.vector.bn_aggr(lnmv[k][:], lnst[k][:]).then_inc(ln_mv[k], 1)

            def normalise(k, t):
                dve.wait_ge(ln_rstd[k], t + 1)
                nc.vector.tensor_scalar(xn[k][:], x[:, t, :], lnmv[k][:, 0:1], lnrs[k][:], ALU.subtract,
                                        ALU.mult).then_inc(ln_done[k], 1)

            def add_to_x(t, ready, product, done):
                dve.wait_ge(ready, t + 1)
                nc.vector.tensor_tensor(x[:, t, :], x[:, t, :], product, ALU.add).then_inc(done, 1)

            def route_best(k, t):
                pass_when(dve, rt_mm[k], t + 1)
                nc.vector.max(gmax[k][:], logits[k]).then_inc(rt_max[k], 1)
                pass_when(dve, rt_max[k], t + 1)
                nc.vector.max_index(gidx[k][:], gmax[k][:], logits[k]).then_inc(rt_idx[k], 1)
                nc.vector.tensor_scalar(glog[k][:], logits[k], gmax[k][:, 0:1], None,
                                        ALU.subtract).then_inc(rt_log[k], 1)

            def route_rec(k, t):
                dve.wait_ge(rt_exp[k], t + 1)
                nc.vector.reciprocal(grec[k][:], gsum[k][:]).then_inc(rt_rec[k], 1)

            def find_best(pair, half, t):
                g = pair // 2
                if pair == 0 and half == 0:
                    if not (isinstance(t, int) and t == 0):
                        pass_when(dve, best_found, HEADS * t)
                    dve.sem_clear(step)
                if pair % 2 == 0 and half == 0:
                    pass_when(dve, s1_act, GROUPS * t + g + 1)
                heads = (2 * pair, 2 * pair + 1)
                for r in (0, 1) if half == 0 else (2, 3):
                    n = (pair * 4 + r) * 4 - 2 * pair
                    for j, h in enumerate(heads):
                        cols = slice((h % HG) * KEYS, (h % HG + 1) * KEYS)
                        if r > 0:
                            dve.wait_ge(step, n + j - 1)
                        nc.vector.max((topr if r else top1)[:, h, :], sw[g][:, 1 if r else 0, cols]).then_inc(step, 1)
                    for j, h in enumerate(heads):
                        cols = slice((h % HG) * KEYS, (h % HG + 1) * KEYS)
                        dve.wait_ge(step, n + 1 + j)
                        nc.vector.match_replace(sw[g][:, 1, cols], in_to_replace=(topr if r else top1)[:, h, :],
                                                in_values=sw[g][:, 1 if r else 0, cols],
                                                imm_value=TAKEN).then_inc(step if r < 3 else best_found, 1)

            def context(t):
                dve.wait_ge(pv_mm, GROUPS * (t + 1))
                nc.vector.reciprocal(rden[:], pv_out[:, :, HD]).then_inc(den_rec, 1)
                dve.wait_ge(den_rec, t + 1)
                nc.vector.tensor_tensor(cx[:], pv_out[:, :, 0:HD], rden[:].unsqueeze(2).to_broadcast([P, HEADS, HD]),
                                        ALU.mult).then_inc(cx_set, 1)

            def combine1(t):
                dve.wait_ge(cnt_mm, t + 1)
                nc.vector.scalar_tensor_tensor(keep[:], count_ps, CAPACITY, gmask[1][:], ALU.is_le,
                                               ALU.mult).then_inc(keep_set, 1)
                dve.wait_ge(keep_set, t + 1)
                nc.vector.scalar_tensor_tensor(tg[:], gexp[1][:], grec[1][:], keep[:], ALU.mult, ALU.mult,
                                               accum_out=tgs[:]).then_inc(tg_set, 1)
                dve.wait_ge(tg_set, t + 1)
                nc.vector.tensor_scalar(tge[:], tgs[:], 1e-6, None, ALU.add).then_inc(tge_set, 1)
                dve.wait_ge(tge_set, t + 1)
                nc.vector.reciprocal(tgr[:], tge[:]).then_inc(tgr_set, 1)
                dve.wait_ge(tgr_set, t + 1)
                nc.vector.tensor_scalar(c1[:], tg[:], tgr[:], None, ALU.mult).then_inc(c1_set, 1)

            def body(i):
                a, b, c, d, m = i + 2, i + 1, i, i - 1, i - 2
                if isinstance(i, int) and i == -2:
                    values0()
                if isinstance(i, int) and i == -2:
                    split_bias()
                if isinstance(i, int) and i == -1:
                    values1()
                if real(c):
                    find_best(0, 0, c)
                if real(b):
                    route_rec(0, b)
                if real(c):
                    find_best(0, 1, c)
                    find_best(1, 0, c)
                    find_best(1, 1, c)
                if real(d):
                    context(d)
                if real(c):
                    find_best(2, 0, c)
                if real(a):
                    stats(0, a)
                if real(c):
                    find_best(2, 1, c)
                if real(d):
                    add_to_x(d, o1_mm, pD[:, 128:256], x_attn1)
                    stats(3, d)
                if real(c):
                    find_best(3, 0, c)
                if real(a):
                    normalise(0, a)
                if real(c):
                    find_best(3, 1, c)
                if real(d):
                    normalise(3, d)
                if real(c):
                    find_best(4, 0, c)
                if real(b):
                    add_to_x(b, y0_mm, pB[:, 128:256], x_moe0)
                    stats(2, b)
                if real(c):
                    find_best(4, 1, c)
                if real(d):
                    route_best(1, d)
                if real(c):
                    find_best(5, 0, c)
                if real(b):
                    normalise(2, b)
                if real(a):
                    add_to_x(a, o0_mm, pA[:, 384:512], x_attn0)
                    stats(1, a)
                if real(c):
                    find_best(5, 1, c)
                if real(d):
                    route_rec(1, d)
                if real(c):
                    find_best(6, 0, c)
                if real(a):
                    normalise(1, a)
                if real(c):
                    find_best(6, 1, c)
                if real(d):
                    combine1(d)
                if real(c):
                    find_best(7, 0, c)
                if real(a):
                    route_best(0, a)
                if real(c):
                    find_best(7, 1, c)
            iterations(dve, body)

        @block.scalar
        def _(act):
            act.wait_ge(kv_mm, 1)
            for b in range(B):
                part = slice(b * QK, (b + 1) * QK)
                nc.scalar.activation(k0[part], R0[part, 0:KEYS], ACT.Identity,
                                     bias=e("bk0")[part]).then_inc(kv_act, 1)
            nc.scalar.activation(qsel_bias[:], e("sel")[0:2 * QK], ACT.Identity,
                                 scale=e("bq0")[0:2 * QK]).then_inc(kv_act, 1)

            def keys1():
                act.wait_ge(kv_mm, 2)
                nc.scalar.activation(k1[:].rearrange("p b k -> p (b k)"), W[0][:, 0:B * KEYS], ACT.Identity,
                                     bias=l("bk1")).then_inc(kv_act, 1)

            def xT_copy(k, t):
                act.wait_ge(xT_mm[k], t + 1)
                nc.scalar.activation(xT[k][:], xT_ps[k], ACT.Identity).then_inc(xT_in[k], 1)

            def attn0_q(t):
                if isinstance(t, int):
                    act.wait_ge(kv_act, 3)
                pass_when(act, q0_mm, t + 1)
                nc.scalar.activation(q0[:], pA[0:2 * QK, 128:256], ACT.Identity, scale=e("sel")[0:2 * QK, t:t + 1]
                                     if isinstance(t, int) else e("sel")[0:2 * QK, bass.ds(t, 1)],
                                     bias=qsel_bias[:, t:t + 1] if isinstance(t, int) else qsel_bias[:, bass.ds(t, 1)]
                                     ).then_inc(q0_act, 1)

            def attn0_tanh(t):
                act.wait_ge(z0_mm, t + 1)
                nc.scalar.activation(th0[:], pA[0:KEYS, 256:384], ACT.Tanh, scale=0.5 * QK ** -0.5).then_inc(tanh0, 1)

            def route_exp(k, t):
                act.wait_ge(rt_log[k], t + 1)
                nc.scalar.activation(gexp[k][:], glog[k][:], ACT.Exp, accum_out=gsum[k][:]).then_inc(rt_exp[k], 1)

            def expert_act(j, t):
                act.wait_ge(h1_mm, 3 * t + j + 1)
                if j == 2 and real(t - 3):
                    act.wait_ge(hid_mm, t - 2)
                if j < 2:
                    nc.scalar.activation(act0[:, 4 * j:4 * j + 4, :].rearrange("p e i -> p (e i)"), R0[:],
                                         ACT.Silu).then_inc(h1_act, 1)
                    act.wait_ge(h3_mm, 2 * t + j + 1)
                    nc.scalar.activation(lin0[:, 4 * j:4 * j + 4, :].rearrange("p e i -> p (e i)"), R1[:],
                                         ACT.Identity).then_inc(h3_act, 1)
                else:
                    nc.scalar.activation(act0[:, E, :], R0[:, 0:INTER], ACT.Silu).then_inc(h1_act, 1)
                    nc.scalar.activation(lin0[:, E, :], R0[:, INTER:2 * INTER], ACT.Identity).then_inc(h3_act, 1)

            def hidden_act(t):
                act.wait_ge(hid_mm, t + 1)
                nc.scalar.activation(hid[:], R0[:, 256:512], ACT.Silu).then_inc(hid_act, 1)

            def c0T_copy(t):
                act.wait_ge(c0T_mm, t + 1)
                nc.scalar.activation(c0T[:], c0T_ps, ACT.Identity).then_inc(c0T_act, 1)

            def gT_copy(j, t):
                act.wait_ge(g0T_mm, 3 * t + j + 1)
                if j == 2 and real(t - 3):
                    act.wait_ge(hidT_mm, t - 2)
                n = 4 if j < 2 else 1
                nc.scalar.activation(g0T[:, 4 * j:4 * j + n, :].rearrange("p e t -> p (e t)"),
                                     (R1, R0, R1)[j][:, 0:n * 128], ACT.Identity).then_inc(g0T_act, 1)

            def hidT_copy(t):
                act.wait_ge(hidT_mm, t + 1)
                nc.scalar.activation(hidT[:].rearrange("p k t -> p (k t)"), R1[:, 256:512],
                                     ACT.Identity).then_inc(hidT_act, 1)

            def y1_copy(n, t):
                act.wait_ge(y1_mm, 2 * t + n + 1)
                nc.scalar.activation(y1[:, n * 512:(n + 1) * 512], (R0, R1)[n][:], ACT.Identity).then_inc(y1_act, 1)

            def q1_copy(t):
                act.wait_ge(q1_mm, t + 1)
                nc.scalar.activation(qT1[:], pB[:, 384:512], ACT.Identity, bias=l("bq1")).then_inc(q1_act, 1)

            def scores_copy(g, t):
                act.wait_ge(s1_mm, GROUPS * t + g + 1)
                if not (isinstance(t, int) and t == 0):
                    act.wait_ge(exps, GROUPS * (t - 1) + g + 1)
                nc.scalar.activation(sw[g][:, 0, :], (R0, R1)[g % 2][:, 0:GK], ACT.Identity,
                                     scale=HD ** -0.5).then_inc(s1_act, 1)

            def weights_exp(g, t):
                act.wait_ge(less_max, GROUPS * t + g + 1)
                if not (isinstance(t, int) and t == 0 and g == 0):
                    act.wait_ge(weights_set, GROUPS * t + g)
                for h in range(HG):
                    cols = slice(h * KEYS, (h + 1) * KEYS)
                    last = nc.scalar.activation(ex[:, :, cols], sw[g][:, :, cols], ACT.Exp,
                                                bias=peak[:, g * HG + h:g * HG + h + 1])
                last.then_inc(exps, 1)

            def pT_copy(g, t):
                act.wait_ge(pT_mm, GROUPS * t + g + 1)
                nc.scalar.activation(pT[g % 2][:], W[g % 2][0:KEYS, :], ACT.Identity).then_inc(pT_act, 1)

            def cxT_copy(t):
                act.wait_ge(cxT_mm, t + 1)
                nc.scalar.activation(cxT[:], pD[:, 0:128], ACT.Identity).then_inc(cxT_act, 1)

            def body(i):
                a, b, c, d, m = i + 2, i + 1, i, i - 1, i - 2
                if isinstance(i, int) and i == -1:
                    keys1()
                if real(d):
                    weights_exp(3, d)
                if real(c):
                    scores_copy(3, c)
                if real(b):
                    expert_act(0, b)
                if real(d):
                    pT_copy(3, d)
                if real(b):
                    expert_act(1, b)
                    expert_act(2, b)
                if real(m):
                    hidden_act(m)
                if real(b):
                    c0T_copy(b)
                if real(d):
                    cxT_copy(d)
                if real(c):
                    weights_exp(0, c)
                if real(b):
                    gT_copy(0, b)
                    gT_copy(1, b)
                    gT_copy(2, b)
                if real(m):
                    hidT_copy(m)
                if real(c):
                    pT_copy(0, c)
                if real(a):
                    xT_copy(0, a)
                    attn0_q(a)
                if real(d):
                    xT_copy(3, d)
                if real(c):
                    weights_exp(1, c)
                if real(a):
                    attn0_tanh(a)
                if real(m):
                    y1_copy(0, m)
                    y1_copy(1, m)
                if real(c):
                    pT_copy(1, c)
                if real(d):
                    route_exp(1, d)
                if real(b):
                    xT_copy(2, b)
                    q1_copy(b)
                if real(c):
                    weights_exp(2, c)
                if real(b):
                    scores_copy(0, b)
                if real(a):
                    xT_copy(1, a)
                if real(b):
                    scores_copy(1, b)
                if real(c):
                    pT_copy(2, c)
                if real(b):
                    scores_copy(2, b)
                if real(a):
                    route_exp(0, a)
            iterations(act, body)

        @block.gpsimd
        def _(pool):
            def spread_keys():
                pool.wait_ge(kv_act, 4)
                for b in range(B):
                    nc.gpsimd.tensor_tensor(kbd[:, b], k1[:, b, :].unsqueeze(1).to_broadcast([D, HEADS, KEYS]),
                                            l("headmask").unsqueeze(2).to_broadcast([D, HEADS, KEYS]),
                                            ALU.mult).then_inc(kv_pool, 1)

            def rstd(k, t):
                pool.wait_ge(ln_mv[k], t + 1)
                nc.gpsimd.tensor_tensor(lnve[k][:], lnmv[k][:, 1:2], eps_t[:], ALU.add).then_inc(ln_ve[k], 1)
                pool.wait_ge(ln_ve[k], t + 1)
                nc.gpsimd.tensor_tensor(lnrs[k][:], lnve[k][:], half_t[:], ALU.pow).then_inc(ln_rstd[k], 1)

            def attn0_sigmoid(t):
                pass_when(pool, tanh0, t + 1)
                nc.gpsimd.tensor_scalar(sg0[:], th0[:], 0.5, 0.5, ALU.mult, ALU.add).then_inc(sigm0, 1)

            def route_mask(k, t):
                pass_when(pool, rt_idx[k], t + 1)
                nc.gpsimd.tensor_copy(gidf[k][:], gidx[k][:, 0:2]).then_inc(rt_idf[k], 1)
                pass_when(pool, rt_idf[k], t + 1)
                for n in range(2):
                    nc.gpsimd.tensor_scalar(gone[k][:, n], e("iota"), gidf[k][:, n:n + 1], None,
                                            ALU.is_equal).then_inc(rt_one[k], 1)
                pool.wait_ge(rt_one[k], 2 * t + 2)
                nc.gpsimd.tensor_tensor(gmask[k][:], gone[k][:, 0], gone[k][:, 1], ALU.add).then_inc(rt_mask[k], 1)

            def combine0(t):
                pass_when(pool, rt_mask[0], t + 1)
                pass_when(pool, rt_rec[0], t + 1)
                nc.gpsimd.tensor_tensor(gone[0][:, 0], gexp[0][:], grec[0][:].to_broadcast([P, E]),
                                        ALU.mult).then_inc(c0_part, 1)
                pool.wait_ge(c0_part, t + 1)
                nc.gpsimd.tensor_tensor(c0[:, 0:E], gone[0][:, 0], gmask[0][:], ALU.mult).then_inc(c0_set, 1)

            def gate_experts(j, t):
                pool.wait_ge(h1_act, 3 * t + j + 1)
                pool.wait_ge(h3_act, 3 * t + j + 1)
                if j == 2:
                    nc.gpsimd.tensor_tensor(g0[:, E], act0[:, E], lin0[:, E], ALU.mult).then_inc(g0_set, 1)
                    return
                part = slice(4 * j, 4 * j + 4)
                nc.gpsimd.tensor_tensor(lin0[:, part], lin0[:, part], act0[:, part], ALU.mult).then_inc(g0_lin, 1)
                pool.wait_ge(g0_lin, 2 * t + j + 1)
                nc.gpsimd.tensor_tensor(g0[:, part], lin0[:, part],
                                        c0[:, part].unsqueeze(2).to_broadcast([P, 4, INTER]),
                                        ALU.mult).then_inc(g0_set, 1)

            def add_bo(t):
                pass_when(pool, ln_done[2], t + 1)
                nc.gpsimd.tensor_tensor(x[:, t, :], x[:, t, :], bo, ALU.add).then_inc(x_bo, 1)

            def less_maximum(g, t):
                pass_when(pool, best_found, HEADS * t + HG * (g + 1))
                nc.gpsimd.tensor_scalar(peak[:, g * HG:(g + 1) * HG], top1[:, g * HG:(g + 1) * HG, 0], -1.0, None,
                                        ALU.mult).then_inc(less_max, 1)

            def keep_best(g, t):
                pool.wait_ge(exps, GROUPS * t + g + 1)
                nc.gpsimd.tensor_tensor(pw[:], ex[:, 0], ex[:, 1], ALU.subtract).then_inc(weights_set, 1)

            def count_kept(t):
                pool.wait_ge(cnt_mm, t + 1)
                nc.gpsimd.tensor_tensor(kept_before[:], kept_before[:], gmask[1][:], ALU.add).then_inc(kept_add, 1)

            def moe1_scale(t):
                pool.wait_ge(c1_set, t + 1)
                pool.wait_ge(y1_act, 2 * t + 2)
                nc.gpsimd.tensor_tensor(y1c[:].rearrange("p (e d) -> p e d", e=E), y1[:].rearrange("p (e d) -> p e d", e=E),
                                        c1[:].unsqueeze(2).to_broadcast([P, E, D]), ALU.mult).then_inc(y1_mul, 1)

            def moe1_add(t):
                pool.wait_ge(y1_mul, t + 1)
                nc.gpsimd.tensor_tensor(s4[:], y1c[:, 0:4 * D], y1c[:, 4 * D:], ALU.add).then_inc(y1_s4, 1)
                pool.wait_ge(y1_s4, t + 1)
                nc.gpsimd.tensor_tensor(s2[:], s4[:, 0:2 * D], s4[:, 2 * D:], ALU.add).then_inc(y1_s2, 1)
                pool.wait_ge(y1_s2, t + 1)
                nc.gpsimd.tensor_tensor(s1[:], s2[:, 0:D], s2[:, D:], ALU.add).then_inc(y1_s1, 1)
                pass_when(pool, y1_s1, t + 1)
                pass_when(pool, stored, 16 * (t + 1))
                nc.gpsimd.tensor_tensor(xo[:], s1[:], x[:, t, :], ALU.add).then_inc(xo_set, 1)

            nc.gpsimd.memset(kept_before[:], 0.0).then_inc(kept_add, 1)
            nc.gpsimd.memset(xo[:], 0.0).then_inc(stored, 16)

            def body(i):
                a, b, c, d, m = i + 2, i + 1, i, i - 1, i - 2
                if isinstance(i, int) and i == -2:
                    pool.wait_ge(consts_set, 5)
                if isinstance(i, int) and i == -1:
                    spread_keys()
                if real(d):
                    less_maximum(3, d)
                if real(b):
                    route_mask(0, b)
                if real(d):
                    keep_best(3, d)
                if real(b):
                    combine0(b)
                    gate_experts(0, b)
                    gate_experts(1, b)
                if real(c):
                    less_maximum(0, c)
                if real(b):
                    gate_experts(2, b)
                if real(a):
                    rstd(0, a)
                if real(c):
                    keep_best(0, c)
                if real(d):
                    rstd(3, d)
                if real(c):
                    less_maximum(1, c)
                    keep_best(1, c)
                if real(b):
                    rstd(2, b)
                if real(a):
                    attn0_sigmoid(a)
                if real(m):
                    moe1_scale(m)
                if real(d):
                    route_mask(1, d)
                if real(a):
                    rstd(1, a)
                if real(b):
                    add_bo(b)
                if real(c):
                    less_maximum(2, c)
                if real(m):
                    moe1_add(m)
                if real(c):
                    keep_best(2, c)
                if real(d):
                    count_kept(d)
            iterations(pool, body)


def kernel(**inputs):
    import numpy as np
    import concourse.bacc as bacc
    from concourse.bass_utils import run_bass_kernel_spmd

    a = {k: np.asarray(v) for k, v in inputs.items()}
    f = np.float32

    def pad(v):
        v = v.reshape(-1, 1) if v.ndim == 1 else v
        return np.concatenate([v, np.zeros((128 - v.shape[0], v.shape[1]), f)]) if v.shape[0] < 128 else v

    batch_rows = np.repeat(np.eye(B, dtype=f), QK, axis=0)
    early = {
        "ident": np.eye(128, dtype=f),
        "ctxT": a["ctx_1024"].reshape(B * KEYS, D).T,
        "wk0": a["L0_xattn_Wk"].T,
        "wq0": np.concatenate([a["L0_xattn_Wq"].T] * 2, axis=1),
        "wv0": a["L0_xattn_Wv"].T,
        "bq0": np.concatenate([a["L0_xattn_bq"]] * 2),
        "bk0": np.concatenate([a["L0_xattn_bk"]] * 2),
        "sel": np.repeat(batch_rows, PER_BATCH, axis=1),
        "iota": np.tile(np.arange(E, dtype=f), (128, 1)),
        "gate": a["L0_ffn_gate_w"].T,
    }
    late = {
        "wq1": a["L1_xattn_Wq"].T,
        "wk1": a["L1_xattn_Wk"].T,
        "wv1": a["L1_xattn_Wv"].T,
        "wo1": a["L1_xattn_Wo"].T,
        "router": a["L1_ffn_w_router"].T,
        "wg": a["L1_ffn_w_gate"].T,
        "triu": np.triu(np.ones((128, 128), f)),
        "ones": np.ones((128, 128), f),
        "headmask": np.repeat(np.eye(HEADS, dtype=f), HD, axis=0),
        "bq1": a["L1_xattn_bq"],
        "bk1": a["L1_xattn_bk"],
        "bias": np.concatenate([a["L0_ffn_b1"].reshape(-1), a["L0_ffn_b3"].reshape(-1), a["L0_ffn_sb1"],
                                a["L0_ffn_sb3"]]).reshape(128, 18),
    }
    arrays = {
        "early": np.concatenate([pad(early[n]) for n, _ in EARLY], axis=1),
        "late": np.concatenate([pad(late[n]) for n, _ in LATE], axis=1),
        "x": a["x"].reshape(TILES, P, D),
        "rows": np.concatenate([a["L0_xattn_bv"], a["L1_xattn_bv"], a["L1_xattn_bo"]]),
        "w1": a["L0_ffn_w1"].transpose(1, 0, 2).reshape(D, E * INTER),
        "w3": a["L0_ffn_w3"].transpose(1, 0, 2).reshape(D, E * INTER),
        "w2": a["L0_ffn_w2"].transpose(1, 0, 2).reshape(INTER, E * D),
        "sw13": np.concatenate([a["L0_ffn_sw1"], a["L0_ffn_sw3"]], axis=1),
        "sw2": a["L0_ffn_sw2"],
        "b2": np.concatenate([a["L0_ffn_b2"], a["L0_ffn_sb2"].reshape(1, D)]),
        "wd": a["L1_ffn_w_down"].transpose(2, 0, 1).reshape(2, 128, E * D).transpose(1, 0, 2),
    }
    nc = bacc.Bacc("TRN2", target_bir_lowering=False, num_devices=1)
    feed, args = {}, []
    for name, v in arrays.items():
        v = np.ascontiguousarray(v)
        feed[name + "_dram"] = v
        args.append(nc.dram_tensor(name + "_dram", v.shape, mybir.dt.from_np(v.dtype), kind="ExternalInput").ap())
    out = nc.dram_tensor("out_dram", (TILES, P, D), F32, kind="ExternalOutput").ap()
    build(nc, *args, out)
    r = run_bass_kernel_spmd(nc, [feed], core_ids=[0])
    return r.results[0]["out_dram"].reshape(B, S, D)
```

```python
from contextlib import ExitStack

import concourse.bass as bass
from concourse import mybir

F32 = mybir.dt.float32
BF16 = mybir.dt.bfloat16
U32 = mybir.dt.uint32
ALU = mybir.AluOpType
ACT = mybir.ActivationFunctionType

B, S, D = 2, 512, 128
KEYS = 77
P = 128
TILES = B * S // P
PER_BATCH = S // P
QK = 32
E = 8
INTER = 128
HIDDEN = 256
HEADS, HD = 16, 8
TOPK = 32
GROUPS = 4
HG = HEADS // GROUPS
GK = HG * KEYS
CAPACITY = float(-(-(B * S * 5) // (E * 4)))
EPS = 1e-5
TAKEN = -3.0e38

EARLY = [("ident", 128), ("ctxT", B * KEYS), ("wk0", QK), ("wq0", 2 * QK), ("wv0", D), ("bq0", 1), ("bk0", 1),
         ("sel", TILES), ("iota", E), ("gate", E)]
LATE = [("wq1", D), ("wk1", D), ("wv1", D), ("wo1", D), ("router", E), ("wg", HIDDEN), ("triu", P), ("ones", P),
        ("headmask", HEADS), ("bq1", 1), ("bk1", 1), ("bias", 18)]
NBIAS = 2 * E * INTER + 2 * INTER


def columns(fields):
    at, where = 0, {}
    for name, width in fields:
        where[name] = (at, at + width)
        at += width
    return where, at


EARLY_AT, EARLY_W = columns(EARLY)
LATE_AT, LATE_W = columns(LATE)


def build(nc, early_d, late_d, x_d, rows_d, w1_d, w3_d, w2_d, sw13_d, sw2_d, b2_d, wd_d, out_d):
    ctx = ExitStack()
    with ctx:
        def sb(name, shape, dt=F32):
            return ctx.enter_context(nc.sbuf_tensor(name, shape, dt))

        def psum(name, cols=512):
            return ctx.enter_context(nc.psum_tensor(name, [128, cols], F32))

        def sem(name):
            return ctx.enter_context(nc.semaphore(name))

        early = sb("early", [128, EARLY_W])
        late = sb("late", [128, LATE_W])

        def e(name):
            a, b = EARLY_AT[name]
            return early[:, a:b]

        def l(name):
            a, b = LATE_AT[name]
            return late[:, a:b]

        ident, ctxT = e("ident"), e("ctxT")
        rows = sb("rows", [128, 3 * D])
        bv0, bv1, bo = rows[:, 0:D], rows[:, D:2 * D], rows[:, 2 * D:3 * D]
        w1 = sb("w1", [D, E * INTER])
        w3 = sb("w3", [D, E * INTER])
        w2 = sb("w2", [INTER, E * D])
        sw13 = sb("shared_w13", [D, 2 * INTER])
        sw2 = sb("shared_w2", [INTER, D])
        b2 = sb("b2", [E + 1, D])
        wd = sb("wd", [128, 2, E * D])
        bias_dram = nc.dram_tensor("bias_parts", [3, NBIAS], BF16, kind="Internal").ap()
        bias_hml = sb("bias_hml", [128, 3, 18], BF16)
        bias_rest = sb("bias_rest", [128, 2, 18])
        bias3 = sb("bias3", [3, NBIAS], BF16)
        ones3 = sb("ones3", [3, P], BF16)
        eps_t = sb("eps_t", [128, 1])
        half_t = sb("half_t", [128, 1])

        k0 = sb("k0", [2 * QK, KEYS])
        v0 = sb("v0", [KEYS, B, D])
        qsel_bias = sb("qsel_bias", [2 * QK, TILES])
        k1 = sb("k1", [D, B, KEYS])
        kbd = sb("kbd", [D, B, HEADS, KEYS])
        v1 = sb("v1", [KEYS, B, HEADS, HD + 1])

        x = sb("x", [P, TILES, D])
        lnst = [sb(f"lnst{k}", [P, 6]) for k in range(4)]
        lnmv = [sb(f"lnmv{k}", [P, 2]) for k in range(4)]
        lnve = [sb(f"lnve{k}", [P, 1]) for k in range(4)]
        lnrs = [sb(f"lnrs{k}", [P, 1]) for k in range(4)]
        xn = [sb(f"xn{k}", [P, D]) for k in range(4)]
        xT = [sb(f"xT{k}", [D, P]) for k in range(4)]
        q0 = sb("q0", [2 * QK, P])
        th0 = sb("th0", [KEYS, P])
        sg0 = sb("sg0", [KEYS, P])
        gmax = [sb(f"gmax{k}", [P, 8]) for k in range(2)]
        gidx = [sb(f"gidx{k}", [P, 8], U32) for k in range(2)]
        gidf = [sb(f"gidf{k}", [P, 2]) for k in range(2)]
        glog = [sb(f"glog{k}", [P, E]) for k in range(2)]
        gexp = [sb(f"gexp{k}", [P, E]) for k in range(2)]
        gsum = [sb(f"gsum{k}", [P, 1]) for k in range(2)]
        grec = [sb(f"grec{k}", [P, 1]) for k in range(2)]
        gone = [sb(f"gone{k}", [P, 2, E]) for k in range(2)]
        gmask = [sb(f"gmask{k}", [P, E]) for k in range(2)]
        c0 = sb("c0", [P, E + 1])
        c0T = sb("c0T", [E + 1, P])
        act0 = sb("act0", [P, E + 1, INTER])
        lin0 = sb("lin0", [P, E + 1, INTER])
        g0 = sb("g0", [P, E + 1, INTER])
        g0T = sb("g0T", [INTER, E + 1, P])
        qT1 = sb("qT1", [D, P])
        sw = [sb(f"scores{g}", [P, 2, GK]) for g in range(GROUPS)]
        top1 = sb("top1", [P, HEADS, 8])
        topr = sb("topr", [P, HEADS, 8])
        peak = sb("peak", [P, HEADS])
        ex = [sb(f"ex{n}", [P, 2, GK]) for n in range(2)]
        pw = [sb(f"pw{n}", [P, GK]) for n in range(2)]
        pT = [sb(f"pT{n}", [KEYS, HG * P]) for n in range(2)]
        rden = sb("rden", [P, HEADS])
        cx = sb("cx", [P, HEADS, HD])
        cxT = sb("cxT", [D, P])
        kept_before = sb("kept_before", [P, E])
        keep = sb("keep", [P, E])
        tg = sb("tg", [P, E])
        tgs = sb("tgs", [P, 1])
        tge = sb("tge", [P, 1])
        tgr = sb("tgr", [P, 1])
        c1 = sb("c1", [P, E])
        hid = sb("hid", [P, HIDDEN])
        hidT = sb("hidT", [128, 2, P])
        y1 = sb("y1", [P, E * D])
        y1c = sb("y1c", [P, E * D])
        s4 = sb("s4", [P, 4 * D])
        s2 = sb("s2", [P, 2 * D])
        s1 = sb("s1", [P, D])
        xo = sb("xo", [P, D])

        pA = psum("pA")
        pB = psum("pB")
        pD = psum("pD")
        pO = psum("pO")
        R0 = psum("R0")
        R1 = psum("R1")
        W = [psum("W0"), psum("W1")]
        pv_out = pO[:, 0:HEADS * (HD + 1)].rearrange("p (h d) -> p h d", h=HEADS)
        logits = [pB[:, 384:392], pD[:, 384:392]]
        c0T_ps = pB[0:E + 1, 0:128]
        count_ps = pD[:, 392:400]
        xT_ps = [pA[:, 0:128], pB[:, 0:128], pB[:, 256:384], pD[:, 256:384]]

        early_in, late_in, x0_in, x_in, rows_in = (sem(n) for n in ("early_in", "late_in", "x0_in", "x_in", "rows_in"))
        w13_in, w2_in, wd_in, bias_out, bias_in = (sem(n) for n in ("w13_in", "w2_in", "wd_in", "bias_out", "bias_in"))
        stored = sem("stored")
        passed = sem("passed")
        consts_set, bias_split, kv_mm, kv_act, kv_dve, kv_pool = (
            sem(n) for n in ("consts_set", "bias_split", "kv_mm", "kv_act", "kv_dve", "kv_pool"))
        ln_stats = [sem(f"ln_stats{k}") for k in range(4)]
        ln_mv = [sem(f"ln_mv{k}") for k in range(4)]
        ln_ve = [sem(f"ln_ve{k}") for k in range(4)]
        ln_rstd = [sem(f"ln_rstd{k}") for k in range(4)]
        ln_done = [sem(f"ln_done{k}") for k in range(4)]
        xT_mm = [sem(f"xT_mm{k}") for k in range(4)]
        xT_in = [sem(f"xT_in{k}") for k in range(4)]
        q0_mm, q0_act, z0_mm, tanh0, sigm0, o0_mm, x_attn0 = (
            sem(n) for n in ("q0_mm", "q0_act", "z0_mm", "tanh0", "sigm0", "o0_mm", "x_attn0"))
        rt_mm, rt_max, rt_idx, rt_log, rt_exp, rt_rec, rt_idf, rt_one, rt_mask = (
            [sem(f"{n}{k}") for k in range(2)] for n in
            ("rt_mm", "rt_max", "rt_idx", "rt_log", "rt_exp", "rt_rec", "rt_idf", "rt_one", "rt_mask"))
        c0_part, c0_set, c0T_mm, c0T_act = (sem(n) for n in ("c0_part", "c0_set", "c0T_mm", "c0T_act"))
        h1_mm, h3_mm, h1_act, h3_act, g0_lin, g0_set, g0T_mm, g0T_act = (
            sem(n) for n in ("h1_mm", "h3_mm", "h1_act", "h3_act", "g0_lin", "g0_set", "g0T_mm", "g0T_act"))
        y0_mm, x_moe0, x_bo = (sem(n) for n in ("y0_mm", "x_moe0", "x_bo"))
        q1_mm, q1_act, s1_mm, s1_act = (sem(n) for n in ("q1_mm", "q1_act", "s1_mm", "s1_act"))
        step, best_found = sem("step"), sem("best_found")
        less_max, exps, weights_set, pT_mm, pT_act, pv_mm = (
            sem(n) for n in ("less_max", "exps", "weights_set", "pT_mm", "pT_act", "pv_mm"))
        den_rec, cx_set, cxT_mm, cxT_act, o1_mm, x_attn1 = (
            sem(n) for n in ("den_rec", "cx_set", "cxT_mm", "cxT_act", "o1_mm", "x_attn1"))
        hid_mm, hid_act, hidT_mm, hidT_act, cnt_mm, kept_add = (
            sem(n) for n in ("hid_mm", "hid_act", "hidT_mm", "hidT_act", "cnt_mm", "kept_add"))
        keep_set, tg_set, tge_set, tgr_set, c1_set = (
            sem(n) for n in ("keep_set", "tg_set", "tge_set", "tgr_set", "c1_set"))
        y1_mm, y1_act, y1_mul, y1_s4, y1_s2, y1_s1, xo_set = (
            sem(n) for n in ("y1_mm", "y1_act", "y1_mul", "y1_s4", "y1_s2", "y1_s1", "xo_set"))

        FIRST, LAST = 3, TILES - 3

        def real(t):
            return not isinstance(t, int) or 0 <= t < TILES

        def pass_when(eng, s, value):
            eng.wait_ge(s, value)
            if not isinstance(value, int):
                eng.sem_inc(passed)

        def iterations(eng, body):
            for i in range(-2, FIRST):
                body(i)
            with eng.Fori(FIRST, LAST + 1) as i:
                body(i)
            for i in range(LAST + 1, TILES + 2):
                body(i)

        block = ctx.enter_context(nc.Block())

        @block.sync
        def _(sp):
            sp.dma_start(early[:], early_d).then_inc(early_in, 16)
            sp.dma_start(x[:, 0, :], x_d[0]).then_inc(x0_in, 16)
            sp.dma_start(rows[:], rows_d.partition_broadcast(128)).then_inc(rows_in, 16)
            sp.dma_start(late[:], late_d).then_inc(late_in, 16)
            sp.dma_start(w1[:], w1_d).then_inc(w13_in, 16)
            sp.dma_start(w3[:], w3_d).then_inc(w13_in, 16)
            sp.dma_start(sw13[:], sw13_d).then_inc(w13_in, 16)
            sp.dma_start(x[:, 1:, :], x_d[1:].rearrange("t p d -> p t d")).then_inc(x_in, 16)
            sp.wait_ge(bias_split, 5)
            sp.dma_start(bias_dram.rearrange("k (p j) -> p k j", j=18), bias_hml[:]).then_inc(bias_out, 16)
            sp.wait_ge(bias_out, 16)
            sp.dma_start(bias3[:], bias_dram).then_inc(bias_in, 16)
            sp.dma_start(w2[:], w2_d).then_inc(w2_in, 16)
            sp.dma_start(sw2[:], sw2_d).then_inc(w2_in, 16)
            sp.dma_start(b2[:], b2_d).then_inc(w2_in, 16)
            sp.dma_start(wd[:], wd_d).then_inc(wd_in, 16)

            def store(t):
                pass_when(sp, xo_set, t + 1)
                sp.dma_start(out_d[t], xo[:]).then_inc(stored, 16)

            def body(i):
                if real(i - 2):
                    store(i - 2)
            iterations(sp, body)
            sp.wait_ge(stored, 16 * (TILES + 1))

        @block.tensor
        def _(pe):
            pe.wait_ge(early_in, 16)
            for b in range(B):
                cb = ctxT[:, b * KEYS:(b + 1) * KEYS]
                nc.tensor.matmul(R0[b * QK:(b + 1) * QK, 0:KEYS], e("wk0"), cb, start=True, stop=True)
                last = nc.tensor.matmul(R1[0:KEYS, b * D:(b + 1) * D], cb, e("wv0"), start=True, stop=True)
            last.then_inc(kv_mm, 1)

            def later_keys():
                pe.wait_ge(late_in, 16)
                nc.tensor.matmul(W[0][:, 0:B * KEYS], l("wk1"), ctxT, start=True, stop=True)
                for b in range(B):
                    last = nc.tensor.matmul(W[1][0:KEYS, b * D:(b + 1) * D], ctxT[:, b * KEYS:(b + 1) * KEYS],
                                            l("wv1"), start=True, stop=True)
                last.then_inc(kv_mm, 1)

            def turn_xn(k, t):
                pe.wait_ge(ln_done[k], t + 1)
                if k < 2 and not (isinstance(t, int) and t == 0):
                    pe.wait_ge((x_attn0, q1_act)[k], t)
                nc.tensor.transpose(xT_ps[k], xn[k][:], ident).then_inc(xT_mm[k], 1)

            def attn0_q(t):
                pe.wait_ge(xT_in[0], t + 1)
                nc.tensor.matmul(pA[0:2 * QK, 128:256], e("wq0"), xT[0][:], start=True, stop=True).then_inc(q0_mm, 1)

            def attn0_z(t):
                pe.wait_ge(q0_act, t + 1)
                if isinstance(t, int):
                    pe.wait_ge(kv_act, 2)
                nc.tensor.matmul(pA[0:KEYS, 256:384], k0[:], q0[:], start=True, stop=True).then_inc(z0_mm, 1)

            def attn0_o(t):
                if isinstance(t, int):
                    pe.wait_ge(kv_dve, 1)
                pe.wait_ge(sigm0, t + 1)
                nc.tensor.matmul(pA[:, 384:512], sg0[:], v0[:, t // PER_BATCH, :],
                                 start=True, stop=True).then_inc(o0_mm, 1)

            def route(k, t):
                pe.wait_ge(xT_in[k * 2 + 1], t + 1)
                nc.tensor.matmul(logits[k], xT[k * 2 + 1][:], e("gate") if k == 0 else l("router"),
                                 start=True, stop=True).then_inc(rt_mm[k], 1)

            def experts_h1(j, t):
                if isinstance(t, int):
                    pe.wait_ge(w13_in, 48)
                    pe.wait_ge(bias_in, 16)
                    pe.wait_ge(consts_set, 5)
                if j == 0:
                    pe.wait_ge(xT_in[1], t + 1)
                if j == 1:
                    pe.wait_ge(h1_act, 3 * t + 1)
                elif isinstance(t, int) and t == 0:
                    pe.wait_ge(kv_act, 2)
                else:
                    pe.wait_ge(s1_act, GROUPS * t - 1)
                cols = slice(j * 512, (j + 1) * 512)
                nc.tensor.matmul(R0[:], ones3[:], bias3[:, cols], start=True, stop=False)
                nc.tensor.matmul(R0[:], xT[1][:], w1[:, cols], start=False, stop=True).then_inc(h1_mm, 1)

            def experts_h3(j, t):
                if isinstance(t, int):
                    pe.wait_ge(w13_in, 48)
                    pe.wait_ge(bias_in, 16)
                if j == 0:
                    pe.wait_ge(xT_in[1], t + 1)
                if j == 1:
                    pe.wait_ge(h3_act, 3 * t + 1)
                elif isinstance(t, int) and t == 0:
                    pe.wait_ge(kv_dve, 1)
                else:
                    pe.wait_ge(s1_act, GROUPS * t)
                cols = slice(E * INTER + j * 512, E * INTER + (j + 1) * 512)
                nc.tensor.matmul(R1[:], ones3[:], bias3[:, cols], start=True, stop=False)
                nc.tensor.matmul(R1[:], xT[1][:], w3[:, j * 512:(j + 1) * 512],
                                 start=False, stop=True).then_inc(h3_mm, 1)

            def shared(t):
                pe.wait_ge(h1_act, 3 * t + 2)
                nc.tensor.matmul(R0[:, 0:256], ones3[:], bias3[:, 2 * E * INTER:], start=True, stop=False)
                nc.tensor.matmul(R0[:, 0:256], xT[1][:], sw13[:], start=False, stop=True).then_inc(h1_mm, 1)

            def hidden(t):
                pe.wait_ge(xT_in[3], t + 1)
                if not real(t + 3):
                    pe.wait_ge(s1_act, GROUPS * TILES)
                    pe.wait_ge(y1_act, 2 * t)
                nc.tensor.matmul(R0[:, 256:512], xT[3][:], l("wg"), start=True, stop=True).then_inc(hid_mm, 1)

            def turn_c0(t):
                pe.wait_ge(c0_set, t + 1)
                nc.tensor.transpose(c0T_ps, c0[:], ident).then_inc(c0T_mm, 1)

            def turn_g(j, t):
                bank = (R1, R0, R1)[j]
                pe.wait_ge(g0_set, 3 * t + j + 1)
                if j == 0:
                    pe.wait_ge(h3_act, 3 * t + 2)
                elif j == 1:
                    pe.wait_ge(h3_act, 3 * t + 3)
                    pe.wait_ge(h1_act, 3 * t + 3)
                    if real(t - 3):
                        pe.wait_ge(hid_act, t - 2)
                else:
                    pe.wait_ge(g0T_act, 3 * t + 1)
                for n in range(4 if j < 2 else 1):
                    last = nc.tensor.transpose(bank[:, n * 128:(n + 1) * 128], g0[:, 4 * j + n, :], ident)
                last.then_inc(g0T_mm, 1)

            def turn_hidden(t):
                pe.wait_ge(hid_act, t + 1)
                if not real(t + 3):
                    pe.wait_ge(y1_act, 2 * t)
                for n in range(2):
                    last = nc.tensor.transpose(R1[:, 256 + n * 128:384 + n * 128], hid[:, n * 128:(n + 1) * 128],
                                               ident)
                last.then_inc(hidT_mm, 1)

            def moe0_out(t):
                if isinstance(t, int):
                    pe.wait_ge(w2_in, 48)
                pe.wait_ge(c0T_act, t + 1)
                nc.tensor.matmul(pB[:, 128:256], c0T[:], b2[:], start=True, stop=False)
                for j in range(3):
                    pe.wait_ge(g0T_act, 3 * t + j + 1)
                    for n in range(4 if j < 2 else 1):
                        w = w2[:, (4 * j + n) * D:(4 * j + n + 1) * D] if j < 2 else sw2[:]
                        last = nc.tensor.matmul(pB[:, 128:256], g0T[:, 4 * j + n, :], w, start=False, stop=(j == 2))
                last.then_inc(y0_mm, 1)

            def counts(t):
                pe.wait_ge(rt_log[1], t + 1)
                pe.wait_ge(rt_mask[1], t + 1)
                nc.tensor.matmul(count_ps, l("triu"), gmask[1][:], start=True, stop=False)
                pe.wait_ge(kept_add, t + 1)
                nc.tensor.matmul(count_ps, l("ones"), kept_before[:], start=False, stop=True).then_inc(cnt_mm, 1)

            def moe1_out(n, t):
                pe.wait_ge(wd_in, 16)
                pe.wait_ge(hidT_act, t + 1)
                if real(t + 3):
                    pe.wait_ge(g0T_act, 3 * (t + 3) + 3)
                for k in range(2):
                    last = nc.tensor.matmul((R0, R1)[n][:], hidT[:, k, :], wd[:, k, n * 512:(n + 1) * 512],
                                            start=(k == 0), stop=(k == 1))
                last.then_inc(y1_mm, 1)

            def queries1(t):
                pe.wait_ge(xT_in[2], t + 1)
                nc.tensor.matmul(pB[:, 384:512], l("wq1"), xT[2][:], start=True, stop=True).then_inc(q1_mm, 1)

            def scores(g, t):
                bank = (R0, R1)[g % 2]
                if isinstance(t, int):
                    pe.wait_ge(kv_pool, 2)
                if g == 0:
                    pe.wait_ge(q1_act, t + 1)
                if g < 2:
                    if real(t - 3):
                        pe.wait_ge(y1_act, 2 * (t - 3) + g + 1)
                    pe.wait_ge(g0T_act, 3 * t + 3)
                else:
                    pe.wait_ge(s1_act, GROUPS * t + g - 1)
                nc.tensor.matmul(bank[:, 0:GK], qT1[:],
                                 kbd[:, t // PER_BATCH, g * HG:(g + 1) * HG, :].rearrange("p h k -> p (h k)"),
                                 start=True, stop=True).then_inc(s1_mm, 1)

            def turn_weights(g, t):
                n = GROUPS * t + g
                pe.wait_ge(weights_set, n + 1)
                if not (isinstance(t, int) and n < 2):
                    pe.wait_ge(pT_act, n - 1)
                for h in range(HG):
                    last = nc.tensor.transpose(W[g % 2][0:KEYS, h * P:(h + 1) * P], pw[g % 2][:, h * KEYS:(h + 1) * KEYS],
                                               ident)
                last.then_inc(pT_mm, 1)

            def weigh_values(g, t):
                if isinstance(t, int):
                    pe.wait_ge(kv_dve, 3)
                if g == 0 and real(t - 1):
                    pe.wait_ge(cx_set, t)
                pe.wait_ge(pT_act, GROUPS * t + g + 1)
                for h in range(HG):
                    last = nc.tensor.matmul(pv_out[:, g * HG + h, :], pT[g % 2][:, h * P:(h + 1) * P],
                                            v1[:, t // PER_BATCH, g * HG + h, :], start=True, stop=True)
                last.then_inc(pv_mm, 1)

            def turn_cx(t):
                if not (isinstance(t, int) and t == 0):
                    pe.wait_ge(keep_set, t)
                pe.wait_ge(cx_set, t + 1)
                nc.tensor.transpose(pD[:, 0:128], cx[:].rearrange("p h d -> p (h d)"), ident).then_inc(cxT_mm, 1)

            def project1(t):
                pe.wait_ge(cxT_act, t + 1)
                nc.tensor.matmul(pD[:, 128:256], cxT[:], l("wo1"), start=True, stop=True).then_inc(o1_mm, 1)

            def body(i):
                ahead2, ahead1, here, behind1, behind2 = i + 2, i + 1, i, i - 1, i - 2
                if isinstance(i, int) and i == -1:
                    later_keys()
                if real(ahead1):
                    turn_xn(1, ahead1)
                if real(here):
                    scores(2, here)
                if real(behind1):
                    turn_weights(2, behind1)
                if real(ahead1):
                    route(0, ahead1)
                if real(here):
                    scores(3, here)
                if real(ahead1):
                    experts_h1(0, ahead1)
                if real(behind1):
                    weigh_values(0, behind1)
                    weigh_values(1, behind1)
                if real(ahead1):
                    experts_h3(0, ahead1)
                    experts_h1(1, ahead1)
                if real(behind1):
                    turn_weights(3, behind1)
                if real(ahead1):
                    turn_c0(ahead1)
                    experts_h3(1, ahead1)
                    shared(ahead1)
                if real(behind2):
                    hidden(behind2)
                if real(ahead2):
                    turn_xn(0, ahead2)
                if real(behind1):
                    weigh_values(2, behind1)
                    weigh_values(3, behind1)
                if real(ahead2):
                    attn0_q(ahead2)
                if real(behind2):
                    counts(behind2)
                if real(ahead1):
                    turn_g(0, ahead1)
                if real(ahead2):
                    attn0_z(ahead2)
                if real(ahead1):
                    turn_g(1, ahead1)
                    turn_g(2, ahead1)
                if real(behind2):
                    turn_hidden(behind2)
                if real(behind1):
                    turn_cx(behind1)
                if real(ahead1):
                    moe0_out(ahead1)
                if real(behind1):
                    project1(behind1)
                if real(ahead2):
                    attn0_o(ahead2)
                if real(behind2):
                    moe1_out(0, behind2)
                if real(here):
                    turn_weights(0, here)
                if real(ahead1):
                    turn_xn(2, ahead1)
                if real(behind2):
                    moe1_out(1, behind2)
                if real(ahead1):
                    queries1(ahead1)
                if real(here):
                    turn_weights(1, here)
                if real(behind1):
                    turn_xn(3, behind1)
                if real(ahead1):
                    scores(0, ahead1)
                if real(behind1):
                    route(1, behind1)
                if real(ahead1):
                    scores(1, ahead1)
            iterations(pe, body)

        @block.vector
        def _(dve):
            nc.vector.memset(eps_t[:], EPS).then_inc(consts_set, 1)
            nc.vector.memset(half_t[:], -0.5).then_inc(consts_set, 1)
            nc.vector.memset(ones3[:], 1.0).then_inc(consts_set, 1)
            nc.vector.memset(c0[:, E:E + 1], 1.0).then_inc(consts_set, 1)
            nc.vector.memset(v1[:, :, :, HD:HD + 1], 1.0).then_inc(consts_set, 1)

            def values0():
                dve.wait_ge(kv_mm, 1)
                dve.wait_ge(rows_in, 16)
                nc.vector.tensor_tensor(v0[:], R1[0:KEYS, 0:B * D].rearrange("p (b d) -> p b d", b=B),
                                        bv0[0:KEYS].unsqueeze(1).to_broadcast([KEYS, B, D]),
                                        ALU.add).then_inc(kv_dve, 1)

            def split_bias():
                dve.wait_ge(late_in, 16)
                nc.vector.tensor_copy(bias_hml[:, 0], l("bias")).then_inc(bias_split, 1)
                dve.wait_ge(bias_split, 1)
                nc.vector.tensor_tensor(bias_rest[:, 0], l("bias"), bias_hml[:, 0], ALU.subtract).then_inc(bias_split, 1)
                dve.wait_ge(bias_split, 2)
                nc.vector.tensor_copy(bias_hml[:, 1], bias_rest[:, 0]).then_inc(bias_split, 1)
                dve.wait_ge(bias_split, 3)
                nc.vector.tensor_tensor(bias_rest[:, 1], bias_rest[:, 0], bias_hml[:, 1],
                                        ALU.subtract).then_inc(bias_split, 1)
                dve.wait_ge(bias_split, 4)
                nc.vector.tensor_copy(bias_hml[:, 2], bias_rest[:, 1]).then_inc(bias_split, 1)

            def values1():
                dve.wait_ge(kv_mm, 2)
                for b in range(B):
                    nc.vector.tensor_tensor(v1[:, b, :, 0:HD],
                                            W[1][0:KEYS, b * D:(b + 1) * D].rearrange("p (h d) -> p h d", h=HEADS),
                                            bv1[0:KEYS].rearrange("p (h d) -> p h d", h=HEADS),
                                            ALU.add).then_inc(kv_dve, 1)

            def stats(k, t):
                if k == 0:
                    if isinstance(t, int):
                        dve.wait_ge(x0_in if t == 0 else x_in, 16)
                else:
                    pass_when(dve, (x_attn0, x_moe0, x_attn1)[k - 1], t + 1)
                nc.vector.bn_stats(lnst[k][:], x[:, t, :]).then_inc(ln_stats[k], 1)

            def moments(k, t):
                pass_when(dve, ln_stats[k], t + 1)
                nc.vector.bn_aggr(lnmv[k][:], lnst[k][:]).then_inc(ln_mv[k], 1)

            def normalise(k, t):
                dve.wait_ge(ln_rstd[k], t + 1)
                nc.vector.tensor_scalar(xn[k][:], x[:, t, :], lnmv[k][:, 0:1], lnrs[k][:], ALU.subtract,
                                        ALU.mult).then_inc(ln_done[k], 1)

            def add_to_x(t, ready, product, done):
                dve.wait_ge(ready, t + 1)
                if done is x_attn1:
                    dve.wait_ge(x_bo, t + 1)
                nc.vector.tensor_tensor(x[:, t, :], x[:, t, :], product, ALU.add).then_inc(done, 1)

            def route_best(k, t):
                pass_when(dve, rt_mm[k], t + 1)
                nc.vector.max(gmax[k][:], logits[k]).then_inc(rt_max[k], 1)

            def route_index(k, t):
                pass_when(dve, rt_max[k], t + 1)
                nc.vector.max_index(gidx[k][:], gmax[k][:], logits[k]).then_inc(rt_idx[k], 1)
                nc.vector.tensor_scalar(glog[k][:], logits[k], gmax[k][:, 0:1], None,
                                        ALU.subtract).then_inc(rt_log[k], 1)

            def route_rec(k, t):
                dve.wait_ge(rt_exp[k], t + 1)
                nc.vector.reciprocal(grec[k][:], gsum[k][:]).then_inc(rt_rec[k], 1)

            def find_best(n32, t):
                pair, r = n32 // 4, n32 % 4
                g = pair // 2
                if n32 == 0:
                    if not (isinstance(t, int) and t == 0):
                        pass_when(dve, best_found, HEADS * t)
                    dve.sem_clear(step)
                if pair % 2 == 0 and r == 0:
                    pass_when(dve, s1_act, GROUPS * t + g + 1)
                heads = (2 * pair, 2 * pair + 1)
                n = (pair * 4 + r) * 4 - 2 * pair
                for j, h in enumerate(heads):
                    cols = slice((h % HG) * KEYS, (h % HG + 1) * KEYS)
                    if r > 0:
                        dve.wait_ge(step, n + j - 1)
                    nc.vector.max((topr if r else top1)[:, h, :], sw[g][:, 1 if r else 0, cols]).then_inc(step, 1)
                for j, h in enumerate(heads):
                    cols = slice((h % HG) * KEYS, (h % HG + 1) * KEYS)
                    dve.wait_ge(step, n + 1 + j)
                    nc.vector.match_replace(sw[g][:, 1, cols], in_to_replace=(topr if r else top1)[:, h, :],
                                            in_values=sw[g][:, 1 if r else 0, cols],
                                            imm_value=TAKEN).then_inc(step if r < 3 else best_found, 1)

            def weight_sums(t):
                dve.wait_ge(pv_mm, GROUPS * (t + 1))
                nc.vector.reciprocal(rden[:], pv_out[:, :, HD]).then_inc(den_rec, 1)

            def context(t):
                dve.wait_ge(den_rec, t + 1)
                nc.vector.tensor_tensor(cx[:], pv_out[:, :, 0:HD], rden[:].unsqueeze(2).to_broadcast([P, HEADS, HD]),
                                        ALU.mult).then_inc(cx_set, 1)

            def keep_within(t):
                dve.wait_ge(cnt_mm, t + 1)
                nc.vector.scalar_tensor_tensor(keep[:], count_ps, CAPACITY, gmask[1][:], ALU.is_le,
                                               ALU.mult).then_inc(keep_set, 1)

            def kept_gates(t):
                dve.wait_ge(rt_rec[1], t + 1)
                dve.wait_ge(keep_set, t + 1)
                nc.vector.scalar_tensor_tensor(tg[:], gexp[1][:], grec[1][:], keep[:], ALU.mult, ALU.mult,
                                               accum_out=tgs[:]).then_inc(tg_set, 1)

            def kept_sum(t):
                dve.wait_ge(tg_set, t + 1)
                nc.vector.tensor_scalar(tge[:], tgs[:], 1e-6, None, ALU.add).then_inc(tge_set, 1)

            def kept_rec(t):
                dve.wait_ge(tge_set, t + 1)
                nc.vector.reciprocal(tgr[:], tge[:]).then_inc(tgr_set, 1)

            def combine1(t):
                dve.wait_ge(tgr_set, t + 1)
                if not (isinstance(t, int) and t == 0):
                    dve.wait_ge(y1_mul, t)
                nc.vector.tensor_scalar(c1[:], tg[:], tgr[:], None, ALU.mult).then_inc(c1_set, 1)

            def body(i):
                ahead2, ahead1, here, behind1, behind2 = i + 2, i + 1, i, i - 1, i - 2
                if isinstance(i, int) and i == -2:
                    values0()
                    split_bias()
                if isinstance(i, int) and i == -1:
                    values1()
                if real(behind1):
                    find_best(28, behind1)
                if real(behind2):
                    normalise(3, behind2)
                if real(behind1):
                    find_best(29, behind1)
                    find_best(30, behind1)
                    find_best(31, behind1)
                if real(ahead2):
                    stats(0, ahead2)
                if real(behind2):
                    route_best(1, behind2)
                if real(ahead1):
                    normalise(1, ahead1)
                if real(ahead2):
                    moments(0, ahead2)
                if real(behind2):
                    route_index(1, behind2)
                if real(here):
                    find_best(0, here)
                    find_best(1, here)
                    find_best(2, here)
                    find_best(3, here)
                    find_best(4, here)
                if real(ahead1):
                    route_best(0, ahead1)
                if real(here):
                    find_best(5, here)
                if real(ahead1):
                    route_index(0, ahead1)
                if real(here):
                    find_best(6, here)
                    find_best(7, here)
                    find_best(8, here)
                    find_best(9, here)
                if real(ahead1):
                    route_rec(0, ahead1)
                if real(here):
                    find_best(10, here)
                if real(ahead2):
                    normalise(0, ahead2)
                if real(here):
                    find_best(11, here)
                    find_best(12, here)
                    find_best(13, here)
                    find_best(14, here)
                    find_best(15, here)
                    find_best(16, here)
                if real(behind1):
                    weight_sums(behind1)
                if real(here):
                    find_best(17, here)
                if real(behind1):
                    context(behind1)
                if real(behind2):
                    keep_within(behind2)
                if real(here):
                    find_best(18, here)
                    find_best(19, here)
                    find_best(20, here)
                    find_best(21, here)
                    find_best(22, here)
                if real(behind2):
                    route_rec(1, behind2)
                if real(here):
                    find_best(23, here)
                if real(ahead1):
                    add_to_x(ahead1, y0_mm, pB[:, 128:256], x_moe0)
                if real(behind1):
                    add_to_x(behind1, o1_mm, pD[:, 128:256], x_attn1)
                if real(ahead1):
                    stats(2, ahead1)
                if real(ahead2):
                    add_to_x(ahead2, o0_mm, pA[:, 384:512], x_attn0)
                if real(behind2):
                    kept_gates(behind2)
                if real(ahead1):
                    moments(2, ahead1)
                if real(behind1):
                    stats(3, behind1)
                if real(ahead2):
                    stats(1, ahead2)
                if real(behind2):
                    kept_sum(behind2)
                if real(here):
                    find_best(24, here)
                if real(behind1):
                    moments(3, behind1)
                if real(ahead2):
                    moments(1, ahead2)
                if real(ahead1):
                    normalise(2, ahead1)
                if real(here):
                    find_best(25, here)
                if real(behind2):
                    kept_rec(behind2)
                if real(here):
                    find_best(26, here)
                if real(behind2):
                    combine1(behind2)
                if real(here):
                    find_best(27, here)
            iterations(dve, body)

        @block.scalar
        def _(act):
            act.wait_ge(kv_mm, 1)
            for b in range(B):
                part = slice(b * QK, (b + 1) * QK)
                nc.scalar.activation(k0[part], R0[part, 0:KEYS], ACT.Identity,
                                     bias=e("bk0")[part]).then_inc(kv_act, 1)
            nc.scalar.activation(qsel_bias[:], e("sel")[0:2 * QK], ACT.Identity,
                                 scale=e("bq0")[0:2 * QK]).then_inc(kv_act, 1)

            def keys1():
                act.wait_ge(kv_mm, 2)
                nc.scalar.activation(k1[:].rearrange("p b k -> p (b k)"), W[0][:, 0:B * KEYS], ACT.Identity,
                                     bias=l("bk1")).then_inc(kv_act, 1)

            def xT_copy(k, t):
                act.wait_ge(xT_mm[k], t + 1)
                nc.scalar.activation(xT[k][:], xT_ps[k], ACT.Identity).then_inc(xT_in[k], 1)

            def attn0_q(t):
                if isinstance(t, int):
                    act.wait_ge(kv_act, 3)
                pass_when(act, q0_mm, t + 1)
                nc.scalar.activation(q0[:], pA[0:2 * QK, 128:256], ACT.Identity, scale=e("sel")[0:2 * QK, t:t + 1]
                                     if isinstance(t, int) else e("sel")[0:2 * QK, bass.ds(t, 1)],
                                     bias=qsel_bias[:, t:t + 1] if isinstance(t, int) else qsel_bias[:, bass.ds(t, 1)]
                                     ).then_inc(q0_act, 1)

            def attn0_tanh(t):
                act.wait_ge(z0_mm, t + 1)
                nc.scalar.activation(th0[:], pA[0:KEYS, 256:384], ACT.Tanh, scale=0.5 * QK ** -0.5).then_inc(tanh0, 1)

            def route_exp(k, t):
                act.wait_ge(rt_log[k], t + 1)
                nc.scalar.activation(gexp[k][:], glog[k][:], ACT.Exp, accum_out=gsum[k][:]).then_inc(rt_exp[k], 1)

            def expert_act(j, t):
                act.wait_ge(h1_mm, 3 * t + j + 1)
                if j == 2 and real(t - 3):
                    act.wait_ge(hid_mm, t - 2)
                if j < 2:
                    nc.scalar.activation(act0[:, 4 * j:4 * j + 4, :].rearrange("p e i -> p (e i)"), R0[:],
                                         ACT.Silu).then_inc(h1_act, 1)
                else:
                    nc.scalar.activation(act0[:, E, :], R0[:, 0:INTER], ACT.Silu).then_inc(h1_act, 1)
                    nc.scalar.activation(lin0[:, E, :], R0[:, INTER:2 * INTER], ACT.Identity).then_inc(h3_act, 1)

            def expert_lin(j, t):
                act.wait_ge(h3_mm, 2 * t + j + 1)
                nc.scalar.activation(lin0[:, 4 * j:4 * j + 4, :].rearrange("p e i -> p (e i)"), R1[:],
                                     ACT.Identity).then_inc(h3_act, 1)

            def hidden_act(t):
                act.wait_ge(hid_mm, t + 1)
                nc.scalar.activation(hid[:], R0[:, 256:512], ACT.Silu).then_inc(hid_act, 1)

            def c0T_copy(t):
                act.wait_ge(c0T_mm, t + 1)
                nc.scalar.activation(c0T[:], c0T_ps, ACT.Identity).then_inc(c0T_act, 1)

            def gT_copy(j, t):
                act.wait_ge(g0T_mm, 3 * t + j + 1)
                if j == 2 and real(t - 3):
                    act.wait_ge(hidT_mm, t - 2)
                n = 4 if j < 2 else 1
                nc.scalar.activation(g0T[:, 4 * j:4 * j + n, :].rearrange("p e t -> p (e t)"),
                                     (R1, R0, R1)[j][:, 0:n * 128], ACT.Identity).then_inc(g0T_act, 1)

            def hidT_copy(t):
                act.wait_ge(hidT_mm, t + 1)
                nc.scalar.activation(hidT[:].rearrange("p k t -> p (k t)"), R1[:, 256:512],
                                     ACT.Identity).then_inc(hidT_act, 1)

            def y1_copy(n, t):
                act.wait_ge(y1_mm, 2 * t + n + 1)
                if not (isinstance(t, int) and t == 0):
                    act.wait_ge(y1_mul, t)
                nc.scalar.activation(y1[:, n * 512:(n + 1) * 512], (R0, R1)[n][:], ACT.Identity).then_inc(y1_act, 1)

            def q1_copy(t):
                act.wait_ge(q1_mm, t + 1)
                nc.scalar.activation(qT1[:], pB[:, 384:512], ACT.Identity, bias=l("bq1")).then_inc(q1_act, 1)

            def scores_copy(g, t):
                act.wait_ge(s1_mm, GROUPS * t + g + 1)
                if not (isinstance(t, int) and t == 0):
                    act.wait_ge(exps, GROUPS * (t - 1) + g + 1)
                nc.scalar.activation(sw[g][:, 0, :], (R0, R1)[g % 2][:, 0:GK], ACT.Identity,
                                     scale=HD ** -0.5).then_inc(s1_act, 1)

            def weights_exp(g, t):
                act.wait_ge(less_max, GROUPS * t + g + 1)
                n = GROUPS * t + g
                if not (isinstance(t, int) and n < 2):
                    act.wait_ge(weights_set, n - 1)
                for h in range(HG):
                    cols = slice(h * KEYS, (h + 1) * KEYS)
                    last = nc.scalar.activation(ex[g % 2][:, :, cols], sw[g][:, :, cols], ACT.Exp,
                                                bias=peak[:, g * HG + h:g * HG + h + 1])
                last.then_inc(exps, 1)

            def pT_copy(g, t):
                n = GROUPS * t + g
                act.wait_ge(pT_mm, n + 1)
                if not (isinstance(t, int) and n < 2):
                    act.wait_ge(pv_mm, n - 1)
                nc.scalar.activation(pT[g % 2][:], W[g % 2][0:KEYS, :], ACT.Identity).then_inc(pT_act, 1)

            def cxT_copy(t):
                act.wait_ge(cxT_mm, t + 1)
                nc.scalar.activation(cxT[:], pD[:, 0:128], ACT.Identity).then_inc(cxT_act, 1)

            def body(i):
                ahead2, ahead1, here, behind1, behind2 = i + 2, i + 1, i, i - 1, i - 2
                if isinstance(i, int) and i == -1:
                    keys1()
                if real(ahead1):
                    xT_copy(1, ahead1)
                if real(here):
                    scores_copy(1, here)
                    scores_copy(2, here)
                    scores_copy(3, here)
                if real(ahead1):
                    route_exp(0, ahead1)
                    expert_act(0, ahead1)
                    expert_lin(0, ahead1)
                    expert_act(1, ahead1)
                if real(behind1):
                    pT_copy(2, behind1)
                    pT_copy(3, behind1)
                if real(ahead1):
                    expert_lin(1, ahead1)
                    c0T_copy(ahead1)
                    expert_act(2, ahead1)
                if real(behind2):
                    hidden_act(behind2)
                if real(ahead2):
                    xT_copy(0, ahead2)
                if real(behind2):
                    route_exp(1, behind2)
                if real(ahead2):
                    attn0_q(ahead2)
                if real(ahead1):
                    gT_copy(0, ahead1)
                if real(ahead2):
                    attn0_tanh(ahead2)
                if real(ahead1):
                    gT_copy(1, ahead1)
                if real(behind1):
                    cxT_copy(behind1)
                if real(behind2):
                    hidT_copy(behind2)
                if real(ahead1):
                    gT_copy(2, ahead1)
                if real(here):
                    weights_exp(0, here)
                    weights_exp(1, here)
                    weights_exp(2, here)
                    pT_copy(0, here)
                if real(behind2):
                    y1_copy(0, behind2)
                if real(ahead1):
                    xT_copy(2, ahead1)
                if real(behind2):
                    y1_copy(1, behind2)
                if real(ahead1):
                    q1_copy(ahead1)
                if real(behind1):
                    xT_copy(3, behind1)
                if real(here):
                    pT_copy(1, here)
                if real(ahead1):
                    scores_copy(0, ahead1)
                if real(here):
                    weights_exp(3, here)
            iterations(act, body)

        @block.gpsimd
        def _(pool):
            def spread_keys():
                pool.wait_ge(kv_act, 4)
                for b in range(B):
                    nc.gpsimd.tensor_tensor(kbd[:, b], k1[:, b, :].unsqueeze(1).to_broadcast([D, HEADS, KEYS]),
                                            l("headmask").unsqueeze(2).to_broadcast([D, HEADS, KEYS]),
                                            ALU.mult).then_inc(kv_pool, 1)

            def rstd(k, t):
                pool.wait_ge(ln_mv[k], t + 1)
                nc.gpsimd.tensor_tensor(lnve[k][:], lnmv[k][:, 1:2], eps_t[:], ALU.add).then_inc(ln_ve[k], 1)
                pool.wait_ge(ln_ve[k], t + 1)
                nc.gpsimd.tensor_tensor(lnrs[k][:], lnve[k][:], half_t[:], ALU.pow).then_inc(ln_rstd[k], 1)

            def attn0_sigmoid(t):
                pass_when(pool, tanh0, t + 1)
                nc.gpsimd.tensor_scalar(sg0[:], th0[:], 0.5, 0.5, ALU.mult, ALU.add).then_inc(sigm0, 1)

            def route_mask(k, t):
                pass_when(pool, rt_idx[k], t + 1)
                nc.gpsimd.tensor_copy(gidf[k][:], gidx[k][:, 0:2]).then_inc(rt_idf[k], 1)
                pass_when(pool, rt_idf[k], t + 1)
                for n in range(2):
                    nc.gpsimd.tensor_scalar(gone[k][:, n], e("iota"), gidf[k][:, n:n + 1], None,
                                            ALU.is_equal).then_inc(rt_one[k], 1)
                pool.wait_ge(rt_one[k], 2 * t + 2)
                nc.gpsimd.tensor_tensor(gmask[k][:], gone[k][:, 0], gone[k][:, 1], ALU.add).then_inc(rt_mask[k], 1)

            def combine0(t):
                pass_when(pool, rt_mask[0], t + 1)
                pass_when(pool, rt_rec[0], t + 1)
                nc.gpsimd.tensor_tensor(gone[0][:, 0], gexp[0][:], grec[0][:].to_broadcast([P, E]),
                                        ALU.mult).then_inc(c0_part, 1)
                pool.wait_ge(c0_part, t + 1)
                nc.gpsimd.tensor_tensor(c0[:, 0:E], gone[0][:, 0], gmask[0][:], ALU.mult).then_inc(c0_set, 1)

            def gate_linear(j, t):
                pool.wait_ge(h1_act, 3 * t + j + 1)
                pool.wait_ge(h3_act, 3 * t + j + 1)
                if j == 2:
                    nc.gpsimd.tensor_tensor(g0[:, E], act0[:, E], lin0[:, E], ALU.mult).then_inc(g0_set, 1)
                    return
                part = slice(4 * j, 4 * j + 4)
                nc.gpsimd.tensor_tensor(lin0[:, part], lin0[:, part], act0[:, part], ALU.mult).then_inc(g0_lin, 1)

            def combine_experts(j, t):
                pool.wait_ge(c0_set, t + 1)
                pool.wait_ge(g0_lin, 2 * t + j + 1)
                part = slice(4 * j, 4 * j + 4)
                nc.gpsimd.tensor_tensor(g0[:, part], lin0[:, part],
                                        c0[:, part].unsqueeze(2).to_broadcast([P, 4, INTER]),
                                        ALU.mult).then_inc(g0_set, 1)

            def add_bo(t):
                pass_when(pool, ln_done[2], t + 1)
                nc.gpsimd.tensor_tensor(x[:, t, :], x[:, t, :], bo, ALU.add).then_inc(x_bo, 1)

            def less_maximum(g, t):
                pass_when(pool, best_found, HEADS * t + HG * (g + 1))
                nc.gpsimd.tensor_scalar(peak[:, g * HG:(g + 1) * HG], top1[:, g * HG:(g + 1) * HG, 0], -1.0, None,
                                        ALU.mult).then_inc(less_max, 1)

            def keep_best(g, t):
                n = GROUPS * t + g
                pool.wait_ge(exps, n + 1)
                if not (isinstance(t, int) and n < 2):
                    pool.wait_ge(pT_mm, n - 1)
                nc.gpsimd.tensor_tensor(pw[g % 2][:], ex[g % 2][:, 0], ex[g % 2][:, 1], ALU.subtract).then_inc(weights_set, 1)

            def count_kept(t):
                pool.wait_ge(cnt_mm, t + 1)
                nc.gpsimd.tensor_tensor(kept_before[:], kept_before[:], gmask[1][:], ALU.add).then_inc(kept_add, 1)

            def moe1_scale(t):
                pool.wait_ge(c1_set, t + 1)
                pool.wait_ge(y1_act, 2 * t + 2)
                nc.gpsimd.tensor_tensor(y1c[:].rearrange("p (e d) -> p e d", e=E), y1[:].rearrange("p (e d) -> p e d", e=E),
                                        c1[:].unsqueeze(2).to_broadcast([P, E, D]), ALU.mult).then_inc(y1_mul, 1)

            def moe1_add(t):
                pool.wait_ge(y1_mul, t + 1)
                nc.gpsimd.tensor_tensor(s4[:], y1c[:, 0:4 * D], y1c[:, 4 * D:], ALU.add).then_inc(y1_s4, 1)

            def moe1_end(t):
                pool.wait_ge(y1_s4, t + 1)
                nc.gpsimd.tensor_tensor(s2[:], s4[:, 0:2 * D], s4[:, 2 * D:], ALU.add).then_inc(y1_s2, 1)
                pool.wait_ge(y1_s2, t + 1)
                nc.gpsimd.tensor_tensor(s1[:], s2[:, 0:D], s2[:, D:], ALU.add).then_inc(y1_s1, 1)
                pass_when(pool, y1_s1, t + 1)
                pass_when(pool, stored, 16 * (t + 1))
                nc.gpsimd.tensor_tensor(xo[:], s1[:], x[:, t, :], ALU.add).then_inc(xo_set, 1)

            nc.gpsimd.memset(kept_before[:], 0.0).then_inc(kept_add, 1)
            nc.gpsimd.memset(xo[:], 0.0).then_inc(stored, 16)

            def body(i):
                ahead2, ahead1, here, behind1, behind2 = i + 2, i + 1, i, i - 1, i - 2
                if isinstance(i, int) and i == -2:
                    pool.wait_ge(consts_set, 5)
                if isinstance(i, int) and i == -1:
                    spread_keys()
                if real(ahead1):
                    route_mask(0, ahead1)
                if real(ahead2):
                    rstd(0, ahead2)
                if real(ahead1):
                    combine0(ahead1)
                    gate_linear(0, ahead1)
                    combine_experts(0, ahead1)
                    gate_linear(1, ahead1)
                    combine_experts(1, ahead1)
                    gate_linear(2, ahead1)
                if real(ahead2):
                    attn0_sigmoid(ahead2)
                if real(behind1):
                    add_bo(behind1)
                if real(here):
                    less_maximum(0, here)
                if real(behind2):
                    count_kept(behind2)
                if real(here):
                    less_maximum(1, here)
                    keep_best(0, here)
                    less_maximum(2, here)
                if real(ahead1):
                    rstd(2, ahead1)
                if real(behind1):
                    rstd(3, behind1)
                if real(here):
                    keep_best(1, here)
                    keep_best(2, here)
                if real(ahead2):
                    rstd(1, ahead2)
                if real(behind2):
                    moe1_scale(behind2)
                if real(here):
                    less_maximum(3, here)
                if real(behind1):
                    route_mask(1, behind1)
                if real(here):
                    keep_best(3, here)
                if real(behind2):
                    moe1_add(behind2)
                    moe1_end(behind2)
            iterations(pool, body)


def kernel(**inputs):
    import numpy as np
    import concourse.bacc as bacc
    from concourse.bass_utils import run_bass_kernel_spmd

    a = {k: np.asarray(v) for k, v in inputs.items()}
    f = np.float32

    def pad(v):
        v = v.reshape(-1, 1) if v.ndim == 1 else v
        return np.concatenate([v, np.zeros((128 - v.shape[0], v.shape[1]), f)]) if v.shape[0] < 128 else v

    batch_rows = np.repeat(np.eye(B, dtype=f), QK, axis=0)
    early = {
        "ident": np.eye(128, dtype=f),
        "ctxT": a["ctx_1024"].reshape(B * KEYS, D).T,
        "wk0": a["L0_xattn_Wk"].T,
        "wq0": np.concatenate([a["L0_xattn_Wq"].T] * 2, axis=1),
        "wv0": a["L0_xattn_Wv"].T,
        "bq0": np.concatenate([a["L0_xattn_bq"]] * 2),
        "bk0": np.concatenate([a["L0_xattn_bk"]] * 2),
        "sel": np.repeat(batch_rows, PER_BATCH, axis=1),
        "iota": np.tile(np.arange(E, dtype=f), (128, 1)),
        "gate": a["L0_ffn_gate_w"].T,
    }
    late = {
        "wq1": a["L1_xattn_Wq"].T,
        "wk1": a["L1_xattn_Wk"].T,
        "wv1": a["L1_xattn_Wv"].T,
        "wo1": a["L1_xattn_Wo"].T,
        "router": a["L1_ffn_w_router"].T,
        "wg": a["L1_ffn_w_gate"].T,
        "triu": np.triu(np.ones((128, 128), f)),
        "ones": np.ones((128, 128), f),
        "headmask": np.repeat(np.eye(HEADS, dtype=f), HD, axis=0),
        "bq1": a["L1_xattn_bq"],
        "bk1": a["L1_xattn_bk"],
        "bias": np.concatenate([a["L0_ffn_b1"].reshape(-1), a["L0_ffn_b3"].reshape(-1), a["L0_ffn_sb1"],
                                a["L0_ffn_sb3"]]).reshape(128, 18),
    }
    arrays = {
        "early": np.concatenate([pad(early[n]) for n, _ in EARLY], axis=1),
        "late": np.concatenate([pad(late[n]) for n, _ in LATE], axis=1),
        "x": a["x"].reshape(TILES, P, D),
        "rows": np.concatenate([a["L0_xattn_bv"], a["L1_xattn_bv"], a["L1_xattn_bo"]]),
        "w1": a["L0_ffn_w1"].transpose(1, 0, 2).reshape(D, E * INTER),
        "w3": a["L0_ffn_w3"].transpose(1, 0, 2).reshape(D, E * INTER),
        "w2": a["L0_ffn_w2"].transpose(1, 0, 2).reshape(INTER, E * D),
        "sw13": np.concatenate([a["L0_ffn_sw1"], a["L0_ffn_sw3"]], axis=1),
        "sw2": a["L0_ffn_sw2"],
        "b2": np.concatenate([a["L0_ffn_b2"], a["L0_ffn_sb2"].reshape(1, D)]),
        "wd": a["L1_ffn_w_down"].transpose(2, 0, 1).reshape(2, 128, E * D).transpose(1, 0, 2),
    }
    nc = bacc.Bacc("TRN2", target_bir_lowering=False, num_devices=1)
    feed, args = {}, []
    for name, v in arrays.items():
        v = np.ascontiguousarray(v)
        feed[name + "_dram"] = v
        args.append(nc.dram_tensor(name + "_dram", v.shape, mybir.dt.from_np(v.dtype), kind="ExternalInput").ap())
    out = nc.dram_tensor("out_dram", (TILES, P, D), F32, kind="ExternalOutput").ap()
    build(nc, *args, out)
    r = run_bass_kernel_spmd(nc, [feed], core_ids=[0])
    return r.results[0]["out_dram"].reshape(B, S, D)
```

```python
from contextlib import ExitStack

import concourse.bass as bass
from concourse import mybir

F32 = mybir.dt.float32
BF16 = mybir.dt.bfloat16
ALU = mybir.AluOpType
ACT = mybir.ActivationFunctionType

B, S, D = 2, 512, 128
KEYS = 77
P = 128
TILES = B * S // P
PER_BATCH = S // P
QK = 32
E = 8
INTER = 128
HIDDEN = 256
HEADS, HD = 16, 8
GROUPS = 4
HG = HEADS // GROUPS
GK = HG * KEYS
CAPACITY = float(-(-(B * S * 5) // (E * 4)))
EPS = 1e-5
TAKEN = -3.0e38

EARLY = [("ident", 128), ("ctxT", B * KEYS), ("wk0", QK), ("wq0", 2 * QK), ("wv0", D), ("bq0", 1), ("bk0", 1),
         ("sel", TILES), ("iota", E), ("gate", E)]
LATE = [("wq1", D), ("wk1", D), ("wv1", D), ("wo1", D), ("router", E), ("wg", HIDDEN), ("triu", P), ("ones", P),
        ("headmask", HEADS), ("bq1", 1), ("bk1", 1), ("bias", 18)]
NBIAS = 2 * E * INTER + 2 * INTER


def columns(fields):
    at, where = 0, {}
    for name, width in fields:
        where[name] = (at, at + width)
        at += width
    return where, at


EARLY_AT, EARLY_W = columns(EARLY)
LATE_AT, LATE_W = columns(LATE)


def build(nc, early_d, late_d, x_d, rows_d, w1_d, w3_d, w2_d, sw13_d, sw2_d, b2_d, wd_d, out_d):
    ctx = ExitStack()
    with ctx:
        def sb(name, shape, dt=F32):
            return ctx.enter_context(nc.sbuf_tensor(name, shape, dt))

        def psum(name, cols=512):
            return ctx.enter_context(nc.psum_tensor(name, [128, cols], F32))

        def sem(name):
            return ctx.enter_context(nc.semaphore(name))

        early = sb("early", [128, EARLY_W])
        late = sb("late", [128, LATE_W])

        def e(name):
            a, b = EARLY_AT[name]
            return early[:, a:b]

        def l(name):
            a, b = LATE_AT[name]
            return late[:, a:b]

        ident, ctxT = e("ident"), e("ctxT")
        rows = sb("rows", [128, 3 * D])
        bv0, bv1, bo = rows[:, 0:D], rows[:, D:2 * D], rows[:, 2 * D:3 * D]
        w1 = sb("w1", [D, E * INTER])
        w3 = sb("w3", [D, E * INTER])
        w2 = sb("w2", [INTER, E * D])
        sw13 = sb("shared_w13", [D, 2 * INTER])
        sw2 = sb("shared_w2", [INTER, D])
        b2 = sb("b2", [E + 1, D])
        wd = sb("wd", [128, 2, E * D])
        bias_dram = nc.dram_tensor("bias_parts", [3, NBIAS], BF16, kind="Internal").ap()
        bias_hml = sb("bias_hml", [128, 3, 18], BF16)
        bias_rest = sb("bias_rest", [128, 2, 18])
        bias3 = sb("bias3", [3, NBIAS], BF16)
        ones3 = sb("ones3", [3, P], BF16)
        warm = sb("warm", [128, 512], BF16)
        eps_t = sb("eps_t", [128, 1])
        half_t = sb("half_t", [128, 1])

        k0 = sb("k0", [2 * QK, KEYS])
        v0 = sb("v0", [KEYS, B, D])
        qsel_bias = sb("qsel_bias", [2 * QK, TILES])
        k1 = sb("k1", [D, B, KEYS])
        kbd = sb("kbd", [D, B, HEADS, KEYS])
        v1 = sb("v1", [KEYS, B, HEADS, HD + 1])

        x = sb("x", [P, TILES, D])
        lnst = [sb(f"lnst{k}", [P, 6]) for k in range(4)]
        lnmv = [sb(f"lnmv{k}", [P, 2]) for k in range(4)]
        lnve = [sb(f"lnve{k}", [P, 1]) for k in range(4)]
        lnrs = [sb(f"lnrs{k}", [P, 1]) for k in range(4)]
        xc = [sb(f"xc{k}", [P, D]) for k in range(4)]
        xn = [sb(f"xn{k}", [P, D]) for k in range(4)]
        xT = [sb(f"xT{k}", [D, P]) for k in range(4)]
        q0 = sb("q0", [2 * QK, P])
        th0 = sb("th0", [KEYS, P])
        sg0 = sb("sg0", [KEYS, P])
        gmax = [sb(f"gmax{k}", [P, 8]) for k in range(2)]
        gneg = [sb(f"gneg{k}", [P, 1]) for k in range(2)]
        grest = [sb(f"grest{k}", [P, E]) for k in range(2)]
        gexp = [sb(f"gexp{k}", [P, E]) for k in range(2)]
        gsum = [sb(f"gsum{k}", [P, 1]) for k in range(2)]
        grec0 = sb("grec0", [P, 1])
        gtwo = [sb(f"gtwo{k}", [P, E]) for k in range(2)]
        gmask = [sb(f"gmask{k}", [P, E]) for k in range(2)]
        c0 = sb("c0", [P, E + 1])
        c0T = sb("c0T", [E + 1, P])
        act0 = sb("act0", [P, E + 1, INTER])
        lin0 = sb("lin0", [P, E + 1, INTER])
        g0 = sb("g0", [P, E + 1, INTER])
        g0T = sb("g0T", [INTER, E + 1, P])
        qT1 = sb("qT1", [D, P])
        sw = [sb(f"scores{g}", [P, 2, GK]) for g in range(GROUPS)]
        top1 = sb("top1", [P, HEADS, 8])
        topr = sb("topr", [P, HEADS, 8])
        peak = sb("peak", [P, HEADS])
        ex = [sb(f"ex{n}", [P, 2, GK]) for n in range(2)]
        pw = [sb(f"pw{n}", [P, GK]) for n in range(2)]
        pT = [sb(f"pT{n}", [KEYS, HG * P]) for n in range(2)]
        rden = sb("rden", [P, HEADS])
        cx = sb("cx", [P, HEADS, HD])
        cxT = sb("cxT", [D, P])
        kept_before = sb("kept_before", [P, E])
        tg = sb("tg", [P, E])
        tgs = sb("tgs", [P, 1])
        tge = sb("tge", [P, 1])
        tgr = sb("tgr", [P, 1])
        c1 = sb("c1", [P, E])
        hid = sb("hid", [P, HIDDEN])
        hidT = sb("hidT", [128, 2, P])
        y1 = sb("y1", [P, E * D])
        s4 = sb("s4", [P, 4 * D])
        s2 = sb("s2", [P, 2 * D])
        s1 = sb("s1", [P, D])
        xo = sb("xo", [P, D])

        pA = psum("pA")
        pB = psum("pB")
        pD = psum("pD")
        pO = psum("pO")
        R0 = psum("R0")
        R1 = psum("R1")
        W = [psum("W0"), psum("W1")]
        pv_out = pO[:, 0:HEADS * (HD + 1)].rearrange("p (h d) -> p h d", h=HEADS)
        logits = [pB[:, 384:392], pD[:, 384:392]]
        c0T_ps = pB[0:E + 1, 0:128]
        count_ps = pD[:, 392:400]
        xT_ps = [pA[:, 0:128], pB[:, 0:128], pB[:, 256:384], pD[:, 256:384]]

        early_in, late_in, x0_in, x_in, rows_in = (sem(n) for n in ("early_in", "late_in", "x0_in", "x_in", "rows_in"))
        w13_in, w2_in, wd_in, bias_out, bias_in = (sem(n) for n in ("w13_in", "w2_in", "wd_in", "bias_out", "bias_in"))
        stored = sem("stored")
        passed = sem("passed")
        warm_set, last_sum = sem("warm_set"), sem("last_sum")
        consts_set, bias_split, kv_mm, kv_act, kv_dve, kv_pool = (
            sem(n) for n in ("consts_set", "bias_split", "kv_mm", "kv_act", "kv_dve", "kv_pool"))
        ln_stats = [sem(f"ln_stats{k}") for k in range(4)]
        ln_mv = [sem(f"ln_mv{k}") for k in range(4)]
        ln_ve = [sem(f"ln_ve{k}") for k in range(4)]
        ln_mid = [sem(f"ln_mid{k}") for k in range(4)]
        ln_rstd = [sem(f"ln_rstd{k}") for k in range(4)]
        ln_done = [sem(f"ln_done{k}") for k in range(4)]
        xT_mm = [sem(f"xT_mm{k}") for k in range(4)]
        xT_in = [sem(f"xT_in{k}") for k in range(4)]
        q0_mm, q0_act, z0_mm, tanh0, sigm0, o0_mm, x_attn0 = (
            sem(n) for n in ("q0_mm", "q0_act", "z0_mm", "tanh0", "sigm0", "o0_mm", "x_attn0"))
        rt_mm, rt_max, rt_pad, rt_neg, rt_exp, rt_rest, rt_mask, rt_two = (
            [sem(f"{n}{k}") for k in range(2)] for n in
            ("rt_mm", "rt_max", "rt_pad", "rt_neg", "rt_exp", "rt_rest", "rt_mask", "rt_two"))
        rt_rec, c0_set, c0T_mm, c0T_act = (sem(n) for n in ("rt_rec", "c0_set", "c0T_mm", "c0T_act"))
        h1_mm, h3_mm, h1_act, h3_act, g0_set, g0T_mm, g0T_act = (
            sem(n) for n in ("h1_mm", "h3_mm", "h1_act", "h3_act", "g0_set", "g0T_mm", "g0T_act"))
        y0_mm, x_moe0, x_bo = (sem(n) for n in ("y0_mm", "x_moe0", "x_bo"))
        q1_mm, q1_act, s1_mm, s1_act = (sem(n) for n in ("q1_mm", "q1_act", "s1_mm", "s1_act"))
        step, best_found = sem("step"), sem("best_found")
        less_max, exps, weights_set, pT_mm, pT_act, pv_mm = (
            sem(n) for n in ("less_max", "exps", "weights_set", "pT_mm", "pT_act", "pv_mm"))
        den_rec, cx_set, cxT_mm, cxT_act, o1_mm, x_attn1 = (
            sem(n) for n in ("den_rec", "cx_set", "cxT_mm", "cxT_act", "o1_mm", "x_attn1"))
        hid_mm, hid_act, hidT_mm, hidT_act, cnt_mm, kept_add = (
            sem(n) for n in ("hid_mm", "hid_act", "hidT_mm", "hidT_act", "cnt_mm", "kept_add"))
        tg_set, tge_set, tgr_set, c1_set = (
            sem(n) for n in ("tg_set", "tge_set", "tgr_set", "c1_set"))
        y1_mm, y1_act, y1_s4, y1_s2, y1_s1, xo_set = (
            sem(n) for n in ("y1_mm", "y1_act", "y1_s4", "y1_s2", "y1_s1", "xo_set"))

        FIRST, LAST = 3, TILES - 3

        def real(t):
            return not isinstance(t, int) or 0 <= t < TILES

        def pass_when(eng, s, value):
            eng.wait_ge(s, value)
            if not isinstance(value, int):
                eng.sem_inc(passed)

        def iterations(eng, start, body, finish):
            for i in range(-2, FIRST):
                start(i)
            with eng.Fori(FIRST, LAST + 1) as i:
                body(i)
            for i in range(LAST + 1, TILES + 2):
                finish(i)

        block = ctx.enter_context(nc.Block())

        @block.sync
        def _(sp):
            sp.dma_start(x[:, 0, :], x_d[0]).then_inc(x0_in, 16)
            sp.dma_start(early[:], early_d).then_inc(early_in, 16)
            sp.dma_start(rows[:], rows_d.partition_broadcast(128)).then_inc(rows_in, 16)
            sp.dma_start(late[:], late_d).then_inc(late_in, 16)
            sp.dma_start(w1[:], w1_d).then_inc(w13_in, 16)
            sp.dma_start(w3[:], w3_d).then_inc(w13_in, 16)
            sp.dma_start(sw13[:], sw13_d).then_inc(w13_in, 16)
            sp.dma_start(x[:, 1:, :], x_d[1:].rearrange("t p d -> p t d")).then_inc(x_in, 16)
            sp.wait_ge(bias_split, 5)
            sp.dma_start(bias_dram.rearrange("k (p j) -> p k j", j=18), bias_hml[:]).then_inc(bias_out, 16)
            sp.wait_ge(bias_out, 16)
            sp.dma_start(bias3[:], bias_dram).then_inc(bias_in, 16)
            sp.dma_start(w2[:], w2_d).then_inc(w2_in, 16)
            sp.dma_start(sw2[:], sw2_d).then_inc(w2_in, 16)
            sp.dma_start(b2[:], b2_d).then_inc(w2_in, 16)
            sp.dma_start(wd[:], wd_d).then_inc(wd_in, 16)

            def store(t):
                pass_when(sp, xo_set, t + 1)
                sp.dma_start(out_d[t], xo[:]).then_inc(stored, 16)

            def body(i):
                if real(i - 2):
                    store(i - 2)
            iterations(sp, body, body, body)
            sp.wait_ge(stored, 16 * (TILES + 1))

        @block.tensor
        def _(pe):
            def warm_up(products):
                pe.wait_ge(warm_set, 1)
                for _ in range(products):
                    nc.tensor.matmul(pO[:], warm[:, 0:128], warm[:], start=True, stop=True)

            def warm_up_first():
                warm_up(8)

            def warm_up_again():
                warm_up(8)

            warm_up(6)
            pe.wait_ge(early_in, 16)
            for b in range(B):
                cb = ctxT[:, b * KEYS:(b + 1) * KEYS]
                nc.tensor.matmul(R0[b * QK:(b + 1) * QK, 0:KEYS], e("wk0"), cb, start=True, stop=True)
                last = nc.tensor.matmul(R1[0:KEYS, b * D:(b + 1) * D], cb, e("wv0"), start=True, stop=True)
            last.then_inc(kv_mm, 1)

            def later_keys():
                pe.wait_ge(late_in, 16)
                nc.tensor.matmul(W[0][:, 0:B * KEYS], l("wk1"), ctxT, start=True, stop=True)
                for b in range(B):
                    last = nc.tensor.matmul(W[1][0:KEYS, b * D:(b + 1) * D], ctxT[:, b * KEYS:(b + 1) * KEYS],
                                            l("wv1"), start=True, stop=True)
                last.then_inc(kv_mm, 1)

            def turn_xn(k, t):
                pe.wait_ge(ln_done[k], t + 1)
                if k < 2 and not (isinstance(t, int) and t == 0):
                    pe.wait_ge((x_attn0, q1_act)[k], t)
                nc.tensor.transpose(xT_ps[k], xn[k][:], ident).then_inc(xT_mm[k], 1)

            def attn0_q(t):
                pe.wait_ge(xT_in[0], t + 1)
                nc.tensor.matmul(pA[0:2 * QK, 128:256], e("wq0"), xT[0][:], start=True, stop=True).then_inc(q0_mm, 1)

            def attn0_z(t):
                pe.wait_ge(q0_act, t + 1)
                if isinstance(t, int):
                    pe.wait_ge(kv_act, 2)
                nc.tensor.matmul(pA[0:KEYS, 256:384], k0[:], q0[:], start=True, stop=True).then_inc(z0_mm, 1)

            def attn0_o(t):
                if isinstance(t, int):
                    pe.wait_ge(kv_dve, 1)
                pe.wait_ge(sigm0, t + 1)
                nc.tensor.matmul(pA[:, 384:512], sg0[:], v0[:, t // PER_BATCH, :],
                                 start=True, stop=True).then_inc(o0_mm, 1)

            def route(k, t):
                pe.wait_ge(xT_in[k * 2 + 1], t + 1)
                nc.tensor.matmul(logits[k], xT[k * 2 + 1][:], e("gate") if k == 0 else l("router"),
                                 start=True, stop=True).then_inc(rt_mm[k], 1)

            def experts_h1(j, t):
                if isinstance(t, int):
                    pe.wait_ge(w13_in, 48)
                    pe.wait_ge(bias_in, 16)
                    pe.wait_ge(consts_set, 5)
                if j == 0:
                    pe.wait_ge(xT_in[1], t + 1)
                if j == 1:
                    pe.wait_ge(h1_act, 3 * t + 1)
                elif isinstance(t, int) and t == 0:
                    pe.wait_ge(kv_act, 2)
                else:
                    pe.wait_ge(s1_act, GROUPS * t - 1)
                cols = slice(j * 512, (j + 1) * 512)
                nc.tensor.matmul(R0[:], ones3[:], bias3[:, cols], start=True, stop=False)
                nc.tensor.matmul(R0[:], xT[1][:], w1[:, cols], start=False, stop=True).then_inc(h1_mm, 1)

            def experts_h3(j, t):
                if isinstance(t, int):
                    pe.wait_ge(w13_in, 48)
                    pe.wait_ge(bias_in, 16)
                if j == 0:
                    pe.wait_ge(xT_in[1], t + 1)
                if j == 1:
                    pe.wait_ge(h3_act, 3 * t + 1)
                elif isinstance(t, int) and t == 0:
                    pe.wait_ge(kv_dve, 1)
                else:
                    pe.wait_ge(s1_act, GROUPS * t)
                cols = slice(E * INTER + j * 512, E * INTER + (j + 1) * 512)
                nc.tensor.matmul(R1[:], ones3[:], bias3[:, cols], start=True, stop=False)
                nc.tensor.matmul(R1[:], xT[1][:], w3[:, j * 512:(j + 1) * 512],
                                 start=False, stop=True).then_inc(h3_mm, 1)

            def shared(t):
                pe.wait_ge(h1_act, 3 * t + 2)
                nc.tensor.matmul(R0[:, 0:256], ones3[:], bias3[:, 2 * E * INTER:], start=True, stop=False)
                nc.tensor.matmul(R0[:, 0:256], xT[1][:], sw13[:], start=False, stop=True).then_inc(h1_mm, 1)

            def hidden(t):
                pe.wait_ge(xT_in[3], t + 1)
                if not real(t + 3):
                    pe.wait_ge(s1_act, GROUPS * TILES)
                    pe.wait_ge(y1_act, 2 * t)
                nc.tensor.matmul(R0[:, 256:512], xT[3][:], l("wg"), start=True, stop=True).then_inc(hid_mm, 1)

            def turn_c0(t):
                pe.wait_ge(c0_set, t + 1)
                nc.tensor.transpose(c0T_ps, c0[:], ident).then_inc(c0T_mm, 1)

            def turn_g(j, t):
                bank = (R1, R0, R1)[j]
                pe.wait_ge(g0_set, 3 * t + j + 1)
                if j == 0:
                    pe.wait_ge(h3_act, 3 * t + 2)
                elif j == 1:
                    pe.wait_ge(h3_act, 3 * t + 3)
                    pe.wait_ge(h1_act, 3 * t + 3)
                    if real(t - 3):
                        pe.wait_ge(hid_act, t - 2)
                else:
                    pe.wait_ge(g0T_act, 3 * t + 1)
                for n in range(4 if j < 2 else 1):
                    last = nc.tensor.transpose(bank[:, n * 128:(n + 1) * 128], g0[:, 4 * j + n, :], ident)
                last.then_inc(g0T_mm, 1)

            def turn_hidden(t):
                pe.wait_ge(hid_act, t + 1)
                if not real(t + 3):
                    pe.wait_ge(y1_act, 2 * t)
                for n in range(2):
                    last = nc.tensor.transpose(R1[:, 256 + n * 128:384 + n * 128], hid[:, n * 128:(n + 1) * 128],
                                               ident)
                last.then_inc(hidT_mm, 1)

            def moe0_out(t):
                if isinstance(t, int):
                    pe.wait_ge(w2_in, 48)
                pe.wait_ge(c0T_act, t + 1)
                nc.tensor.matmul(pB[:, 128:256], c0T[:], b2[:], start=True, stop=False)
                for j in range(3):
                    pe.wait_ge(g0T_act, 3 * t + j + 1)
                    for n in range(4 if j < 2 else 1):
                        w = w2[:, (4 * j + n) * D:(4 * j + n + 1) * D] if j < 2 else sw2[:]
                        last = nc.tensor.matmul(pB[:, 128:256], g0T[:, 4 * j + n, :], w, start=False, stop=(j == 2))
                last.then_inc(y0_mm, 1)

            def counts(t):
                pe.wait_ge(rt_exp[1], t + 1)
                pe.wait_ge(rt_mask[1], t + 1)
                nc.tensor.matmul(count_ps, l("triu"), gmask[1][:], start=True, stop=False)
                pe.wait_ge(kept_add, t + 1)
                nc.tensor.matmul(count_ps, l("ones"), kept_before[:], start=False, stop=True).then_inc(cnt_mm, 1)

            def moe1_out(n, t):
                pe.wait_ge(wd_in, 16)
                pe.wait_ge(hidT_act, t + 1)
                if real(t + 3):
                    pe.wait_ge(g0T_act, 3 * (t + 3) + 3)
                for k in range(2):
                    last = nc.tensor.matmul((R0, R1)[n][:], hidT[:, k, :], wd[:, k, n * 512:(n + 1) * 512],
                                            start=(k == 0), stop=(k == 1))
                last.then_inc(y1_mm, 1)

            def queries1(t):
                pe.wait_ge(xT_in[2], t + 1)
                nc.tensor.matmul(pB[:, 384:512], l("wq1"), xT[2][:], start=True, stop=True).then_inc(q1_mm, 1)

            def scores(g, t):
                bank = (R0, R1)[g % 2]
                if isinstance(t, int):
                    pe.wait_ge(kv_pool, 2)
                if g == 0:
                    pe.wait_ge(q1_act, t + 1)
                if g < 2:
                    if real(t - 3):
                        pe.wait_ge(y1_act, 2 * (t - 3) + g + 1)
                    pe.wait_ge(g0T_act, 3 * t + 3)
                else:
                    pe.wait_ge(s1_act, GROUPS * t + g - 1)
                nc.tensor.matmul(bank[:, 0:GK], qT1[:],
                                 kbd[:, t // PER_BATCH, g * HG:(g + 1) * HG, :].rearrange("p h k -> p (h k)"),
                                 start=True, stop=True).then_inc(s1_mm, 1)

            def turn_weights(g, t):
                n = GROUPS * t + g
                pe.wait_ge(weights_set, n + 1)
                if not (isinstance(t, int) and n < 2):
                    pe.wait_ge(pT_act, n - 1)
                for h in range(HG):
                    last = nc.tensor.transpose(W[g % 2][0:KEYS, h * P:(h + 1) * P], pw[g % 2][:, h * KEYS:(h + 1) * KEYS],
                                               ident)
                last.then_inc(pT_mm, 1)

            def weigh_values(g, t):
                if isinstance(t, int):
                    pe.wait_ge(kv_dve, 3)
                if g == 0 and real(t - 1):
                    pe.wait_ge(cx_set, t)
                pe.wait_ge(pT_act, GROUPS * t + g + 1)
                for h in range(HG):
                    last = nc.tensor.matmul(pv_out[:, g * HG + h, :], pT[g % 2][:, h * P:(h + 1) * P],
                                            v1[:, t // PER_BATCH, g * HG + h, :], start=True, stop=True)
                last.then_inc(pv_mm, 1)

            def turn_cx(t):
                if not (isinstance(t, int) and t == 0):
                    pe.wait_ge(tg_set, t)
                pe.wait_ge(cx_set, t + 1)
                nc.tensor.transpose(pD[:, 0:128], cx[:].rearrange("p h d -> p (h d)"), ident).then_inc(cxT_mm, 1)

            def project1(t):
                pe.wait_ge(cxT_act, t + 1)
                nc.tensor.matmul(pD[:, 128:256], cxT[:], l("wo1"), start=True, stop=True).then_inc(o1_mm, 1)

            def start(i):
                ahead2, ahead1, here, behind1, behind2 = i + 2, i + 1, i, i - 1, i - 2
                if i == -1:
                    later_keys()
                if real(ahead1):
                    route(0, ahead1)
                if real(here):
                    scores(3, here)
                if real(ahead1):
                    experts_h1(0, ahead1)
                if real(behind1):
                    turn_weights(2, behind1)
                if real(behind2):
                    turn_xn(3, behind2)
                if real(behind1):
                    weigh_values(1, behind1)
                if real(ahead1):
                    experts_h3(0, ahead1)
                if real(behind2):
                    route(1, behind2)
                if real(ahead1):
                    experts_h1(1, ahead1)
                    experts_h3(1, ahead1)
                if real(behind1):
                    turn_weights(3, behind1)
                if real(ahead1):
                    shared(ahead1)
                if real(behind2):
                    hidden(behind2)
                if real(ahead2):
                    turn_xn(0, ahead2)
                if real(ahead1):
                    turn_c0(ahead1)
                    turn_g(0, ahead1)
                if real(ahead2):
                    attn0_q(ahead2)
                if real(behind1):
                    weigh_values(2, behind1)
                if real(ahead1):
                    turn_g(1, ahead1)
                if real(behind1):
                    weigh_values(3, behind1)
                if real(ahead1):
                    turn_g(2, ahead1)
                if real(behind2):
                    counts(behind2)
                    turn_hidden(behind2)
                if real(ahead1):
                    moe0_out(ahead1)
                if real(ahead2):
                    attn0_z(ahead2)
                if i == -1:
                    warm_up_again()
                if real(behind1):
                    turn_cx(behind1)
                if real(behind2):
                    moe1_out(0, behind2)
                if real(here):
                    turn_weights(0, here)
                if real(ahead2):
                    attn0_o(ahead2)
                if real(behind1):
                    project1(behind1)
                if real(behind2):
                    moe1_out(1, behind2)
                if real(ahead1):
                    turn_xn(2, ahead1)
                if real(here):
                    weigh_values(0, here)
                if real(ahead1):
                    queries1(ahead1)
                if real(here):
                    turn_weights(1, here)
                if real(ahead1):
                    scores(0, ahead1)
                    scores(1, ahead1)
                if i == -2:
                    warm_up_first()
                if real(ahead2):
                    turn_xn(1, ahead2)
                if real(ahead1):
                    scores(2, ahead1)

            def body(i):
                ahead2, ahead1, here, behind1, behind2 = i + 2, i + 1, i, i - 1, i - 2
                route(0, ahead1)
                turn_xn(3, behind2)
                scores(3, here)
                experts_h1(0, ahead1)
                experts_h3(0, ahead1)
                route(1, behind2)
                turn_weights(2, behind1)
                experts_h1(1, ahead1)
                experts_h3(1, ahead1)
                turn_c0(ahead1)
                shared(ahead1)
                hidden(behind2)
                turn_weights(3, behind1)
                turn_xn(0, ahead2)
                weigh_values(1, behind1)
                attn0_q(ahead2)
                turn_g(0, ahead1)
                weigh_values(2, behind1)
                turn_g(1, ahead1)
                counts(behind2)
                attn0_z(ahead2)
                turn_g(2, ahead1)
                turn_hidden(behind2)
                moe0_out(ahead1)
                weigh_values(3, behind1)
                attn0_o(ahead2)
                moe1_out(0, behind2)
                turn_weights(0, here)
                turn_cx(behind1)
                turn_xn(2, ahead1)
                moe1_out(1, behind2)
                queries1(ahead1)
                project1(behind1)
                turn_weights(1, here)
                scores(0, ahead1)
                turn_xn(1, ahead2)
                weigh_values(0, here)
                scores(1, ahead1)
                scores(2, ahead1)

            def finish(i):
                ahead2, ahead1, here, behind1, behind2 = i + 2, i + 1, i, i - 1, i - 2
                if real(behind1):
                    turn_weights(2, behind1)
                if real(ahead1):
                    route(0, ahead1)
                if real(behind2):
                    turn_xn(3, behind2)
                if real(here):
                    scores(3, here)
                if real(ahead1):
                    experts_h1(0, ahead1)
                    experts_h3(0, ahead1)
                if real(behind1):
                    weigh_values(1, behind1)
                if real(ahead2):
                    turn_xn(0, ahead2)
                if real(behind2):
                    route(1, behind2)
                if real(ahead1):
                    experts_h1(1, ahead1)
                    experts_h3(1, ahead1)
                    shared(ahead1)
                if real(behind2):
                    hidden(behind2)
                    if behind2 == TILES - 1:
                        warm_up(3)
                if real(behind1):
                    turn_weights(3, behind1)
                if real(ahead1):
                    turn_g(0, ahead1)
                if real(behind1):
                    weigh_values(2, behind1)
                    weigh_values(3, behind1)
                if real(ahead1):
                    turn_g(1, ahead1)
                    turn_g(2, ahead1)
                    turn_c0(ahead1)
                if real(behind2):
                    turn_hidden(behind2)
                if real(ahead2):
                    turn_xn(1, ahead2)
                if real(behind2):
                    if behind2 < TILES - 1:
                        counts(behind2)
                if real(ahead1):
                    moe0_out(ahead1)
                if real(behind2):
                    moe1_out(0, behind2)
                if real(behind1):
                    turn_cx(behind1)
                if real(here):
                    turn_weights(0, here)
                if real(ahead1):
                    turn_xn(2, ahead1)
                if real(behind1):
                    project1(behind1)
                if real(ahead1):
                    queries1(ahead1)
                if real(ahead2):
                    attn0_q(ahead2)
                    attn0_o(ahead2)
                if real(behind2):
                    if behind2 == TILES - 1:
                        counts(behind2)
                    moe1_out(1, behind2)
                if real(ahead1):
                    scores(0, ahead1)
                if real(here):
                    turn_weights(1, here)
                    weigh_values(0, here)
                if real(ahead2):
                    attn0_z(ahead2)
                if real(ahead1):
                    scores(1, ahead1)
                    scores(2, ahead1)

            iterations(pe, start, body, finish)

        @block.vector
        def _(dve):
            nc.vector.memset(warm[:], 0.0).then_inc(warm_set, 1)
            nc.vector.memset(eps_t[:], EPS).then_inc(consts_set, 1)
            nc.vector.memset(half_t[:], -0.5).then_inc(consts_set, 1)
            nc.vector.memset(ones3[:], 1.0).then_inc(consts_set, 1)
            nc.vector.memset(c0[:, E:E + 1], 1.0).then_inc(consts_set, 1)
            nc.vector.memset(v1[:, :, :, HD:HD + 1], 1.0).then_inc(consts_set, 1)

            def values0():
                dve.wait_ge(kv_mm, 1)
                dve.wait_ge(rows_in, 16)
                nc.vector.tensor_tensor(v0[:], R1[0:KEYS, 0:B * D].rearrange("p (b d) -> p b d", b=B),
                                        bv0[0:KEYS].unsqueeze(1).to_broadcast([KEYS, B, D]),
                                        ALU.add).then_inc(kv_dve, 1)

            def split_bias():
                dve.wait_ge(late_in, 16)
                nc.vector.tensor_copy(bias_hml[:, 0], l("bias")).then_inc(bias_split, 1)
                dve.wait_ge(bias_split, 1)
                nc.vector.tensor_tensor(bias_rest[:, 0], l("bias"), bias_hml[:, 0], ALU.subtract).then_inc(bias_split, 1)
                dve.wait_ge(bias_split, 2)
                nc.vector.tensor_copy(bias_hml[:, 1], bias_rest[:, 0]).then_inc(bias_split, 1)
                dve.wait_ge(bias_split, 3)
                nc.vector.tensor_tensor(bias_rest[:, 1], bias_rest[:, 0], bias_hml[:, 1],
                                        ALU.subtract).then_inc(bias_split, 1)
                dve.wait_ge(bias_split, 4)
                nc.vector.tensor_copy(bias_hml[:, 2], bias_rest[:, 1]).then_inc(bias_split, 1)

            def values1():
                dve.wait_ge(kv_mm, 2)
                for b in range(B):
                    nc.vector.tensor_tensor(v1[:, b, :, 0:HD],
                                            W[1][0:KEYS, b * D:(b + 1) * D].rearrange("p (h d) -> p h d", h=HEADS),
                                            bv1[0:KEYS].rearrange("p (h d) -> p h d", h=HEADS),
                                            ALU.add).then_inc(kv_dve, 1)

            def stats(k, t):
                if k == 0:
                    if isinstance(t, int):
                        dve.wait_ge(x0_in if t == 0 else x_in, 16)
                else:
                    pass_when(dve, (x_attn0, x_moe0, x_attn1)[k - 1], t + 1)
                nc.vector.bn_stats(lnst[k][:], x[:, t, :]).then_inc(ln_stats[k], 1)

            def moments(k, t):
                pass_when(dve, ln_stats[k], t + 1)
                nc.vector.bn_aggr(lnmv[k][:], lnst[k][:]).then_inc(ln_mv[k], 1)

            def add_to_x(t, ready, product, done):
                dve.wait_ge(ready, t + 1)
                if done is x_attn1:
                    dve.wait_ge(x_bo, t + 1)
                nc.vector.tensor_tensor(x[:, t, :], x[:, t, :], product, ALU.add).then_inc(done, 1)

            def route_best(k, t):
                pass_when(dve, rt_mm[k], t + 1)
                nc.vector.max(gmax[k][:], logits[k]).then_inc(rt_max[k], 1)

            def route_rest(k, t):
                pass_when(dve, rt_pad[k], t + 1)
                nc.vector.match_replace(grest[k][:], in_to_replace=gmax[k][:], in_values=logits[k],
                                        imm_value=TAKEN).then_inc(rt_rest[k], 1)

            def route_rec(t):
                dve.wait_ge(rt_exp[0], t + 1)
                nc.vector.reciprocal(grec0[:], gsum[0][:]).then_inc(rt_rec, 1)

            def find_best(n32, t):
                pair, r = n32 // 4, n32 % 4
                g = pair // 2
                if n32 == 0:
                    if not (isinstance(t, int) and t == 0):
                        pass_when(dve, best_found, HEADS * t)
                    dve.sem_clear(step)
                if pair % 2 == 0 and r == 0:
                    pass_when(dve, s1_act, GROUPS * t + g + 1)
                heads = (2 * pair, 2 * pair + 1)
                n = (pair * 4 + r) * 4 - 2 * pair
                for j, h in enumerate(heads):
                    cols = slice((h % HG) * KEYS, (h % HG + 1) * KEYS)
                    if r > 0:
                        dve.wait_ge(step, n + j - 1)
                    nc.vector.max((topr if r else top1)[:, h, :], sw[g][:, 1 if r else 0, cols]).then_inc(step, 1)
                for j, h in enumerate(heads):
                    cols = slice((h % HG) * KEYS, (h % HG + 1) * KEYS)
                    dve.wait_ge(step, n + 1 + j)
                    nc.vector.match_replace(sw[g][:, 1, cols], in_to_replace=(topr if r else top1)[:, h, :],
                                            in_values=sw[g][:, 1 if r else 0, cols],
                                            imm_value=TAKEN).then_inc(step if r < 3 else best_found, 1)

            def weight_sums(t):
                dve.wait_ge(pv_mm, GROUPS * (t + 1))
                nc.vector.reciprocal(rden[:], pv_out[:, :, HD]).then_inc(den_rec, 1)

            def context(t):
                dve.wait_ge(den_rec, t + 1)
                nc.vector.tensor_tensor(cx[:], pv_out[:, :, 0:HD], rden[:].unsqueeze(2).to_broadcast([P, HEADS, HD]),
                                        ALU.mult).then_inc(cx_set, 1)

            def keep_within(t):
                dve.wait_ge(rt_two[1], t + 1)
                dve.wait_ge(cnt_mm, t + 1)
                nc.vector.scalar_tensor_tensor(tg[:], count_ps, CAPACITY, gtwo[1][:], ALU.is_le,
                                               ALU.mult, accum_out=tgs[:]).then_inc(tg_set, 1)

            def kept_rec(t):
                dve.wait_ge(tge_set, t + 1)
                nc.vector.reciprocal(tgr[:], tge[:]).then_inc(tgr_set, 1)

            def gate_experts(j, t):
                if not (isinstance(t, int) and t == 0):
                    return
                dve.wait_ge(h1_act, j + 1)
                dve.wait_ge(h3_act, j + 1)
                part = slice(4 * j, min(4 * j + 4, E + 1))
                nc.vector.tensor_tensor(g0[:, part], lin0[:, part], act0[:, part], ALU.mult).then_inc(g0_set, 1)

            def moe1_sum(n, t):
                if not (isinstance(t, int) and t == TILES - 1):
                    return
                h = 4 * n * D
                dve.wait_ge(y1_act, 2 * t + n + 1)
                nc.vector.tensor_tensor(y1[:, h:h + 2 * D], y1[:, h:h + 2 * D], y1[:, h + 2 * D:h + 4 * D],
                                        ALU.add).then_inc(last_sum, 1)
                dve.wait_ge(last_sum, 2 * n + 1)
                nc.vector.tensor_tensor(y1[:, h:h + D], y1[:, h:h + D], y1[:, h + D:h + 2 * D],
                                        ALU.add).then_inc(last_sum, 1)

            def moe1_last(t):
                if not (isinstance(t, int) and t == TILES - 1):
                    return
                dve.wait_ge(last_sum, 4)
                nc.vector.tensor_tensor(y1[:, 0:D], y1[:, 0:D], y1[:, 4 * D:5 * D], ALU.add).then_inc(last_sum, 1)
                dve.wait_ge(last_sum, 5)
                dve.wait_ge(stored, 16 * (t + 1))
                nc.vector.tensor_tensor(xo[:], y1[:, 0:D], x[:, t, :], ALU.add).then_inc(xo_set, 1)

            def start(i):
                ahead2, ahead1, here, behind1, behind2 = i + 2, i + 1, i, i - 1, i - 2
                if real(ahead2):
                    stats(0, ahead2)
                if real(here):
                    find_best(0, here)
                    find_best(1, here)
                if real(ahead2):
                    moments(0, ahead2)
                if real(ahead1):
                    route_best(0, ahead1)
                if real(here):
                    find_best(2, here)
                    find_best(3, here)
                if real(ahead1):
                    route_rest(0, ahead1)
                if real(here):
                    find_best(4, here)
                if real(ahead1):
                    route_rec(ahead1)
                if real(here):
                    find_best(5, here)
                    find_best(6, here)
                if real(behind2):
                    route_best(1, behind2)
                if real(here):
                    find_best(7, here)
                    find_best(8, here)
                    find_best(9, here)
                    find_best(10, here)
                if real(ahead1):
                    gate_experts(0, ahead1)
                if real(here):
                    find_best(11, here)
                if real(behind2):
                    route_rest(1, behind2)
                if real(here):
                    find_best(12, here)
                    find_best(13, here)
                    find_best(14, here)
                    find_best(15, here)
                    find_best(16, here)
                    find_best(17, here)
                    find_best(18, here)
                if i == -1:
                    values1()
                if real(here):
                    find_best(19, here)
                if real(behind1):
                    weight_sums(behind1)
                if real(here):
                    find_best(20, here)
                if real(behind1):
                    context(behind1)
                if real(ahead1):
                    gate_experts(1, ahead1)
                if i == -2:
                    split_bias()
                if real(behind2):
                    keep_within(behind2)
                if real(here):
                    find_best(21, here)
                    find_best(22, here)
                if real(ahead1):
                    gate_experts(2, ahead1)
                if real(here):
                    find_best(23, here)
                if real(ahead1):
                    add_to_x(ahead1, y0_mm, pB[:, 128:256], x_moe0)
                    stats(2, ahead1)
                if real(behind2):
                    kept_rec(behind2)
                if real(ahead1):
                    moments(2, ahead1)
                if real(here):
                    find_best(24, here)
                if i == -2:
                    values0()
                if real(here):
                    find_best(25, here)
                if real(behind1):
                    add_to_x(behind1, o1_mm, pD[:, 128:256], x_attn1)
                if real(ahead2):
                    add_to_x(ahead2, o0_mm, pA[:, 384:512], x_attn0)
                if real(behind1):
                    stats(3, behind1)
                if real(ahead2):
                    stats(1, ahead2)
                if real(here):
                    find_best(26, here)
                    find_best(27, here)
                if real(ahead2):
                    moments(1, ahead2)
                if real(here):
                    find_best(28, here)
                    find_best(29, here)
                    find_best(30, here)
                if real(behind1):
                    moments(3, behind1)
                if real(here):
                    find_best(31, here)

            def body(i):
                ahead2, ahead1, here, behind1, behind2 = i + 2, i + 1, i, i - 1, i - 2
                find_best(0, here)
                find_best(1, here)
                find_best(2, here)
                route_best(0, ahead1)
                stats(0, ahead2)
                find_best(3, here)
                route_rest(0, ahead1)
                moments(0, ahead2)
                find_best(4, here)
                route_rec(ahead1)
                find_best(5, here)
                find_best(6, here)
                find_best(7, here)
                find_best(8, here)
                route_best(1, behind2)
                find_best(9, here)
                find_best(10, here)
                find_best(11, here)
                find_best(12, here)
                find_best(13, here)
                route_rest(1, behind2)
                find_best(14, here)
                find_best(15, here)
                find_best(16, here)
                find_best(17, here)
                find_best(18, here)
                find_best(19, here)
                keep_within(behind2)
                find_best(20, here)
                find_best(21, here)
                find_best(22, here)
                find_best(23, here)
                find_best(24, here)
                add_to_x(ahead1, y0_mm, pB[:, 128:256], x_moe0)
                kept_rec(behind2)
                stats(2, ahead1)
                moments(2, ahead1)
                add_to_x(ahead2, o0_mm, pA[:, 384:512], x_attn0)
                find_best(25, here)
                weight_sums(behind1)
                stats(1, ahead2)
                moments(1, ahead2)
                context(behind1)
                find_best(26, here)
                find_best(27, here)
                find_best(28, here)
                find_best(29, here)
                find_best(30, here)
                add_to_x(behind1, o1_mm, pD[:, 128:256], x_attn1)
                find_best(31, here)
                stats(3, behind1)
                moments(3, behind1)

            def finish(i):
                ahead2, ahead1, here, behind1, behind2 = i + 2, i + 1, i, i - 1, i - 2
                if real(ahead2):
                    moments(1, ahead2)
                    stats(1, ahead2)
                if real(here):
                    find_best(0, here)
                    find_best(1, here)
                    find_best(2, here)
                    find_best(3, here)
                    find_best(4, here)
                if real(ahead2):
                    add_to_x(ahead2, o0_mm, pA[:, 384:512], x_attn0)
                if real(ahead1):
                    route_best(0, ahead1)
                    route_rest(0, ahead1)
                if real(here):
                    find_best(5, here)
                    find_best(6, here)
                if real(ahead1):
                    route_rec(ahead1)
                if real(here):
                    find_best(7, here)
                    find_best(8, here)
                    find_best(9, here)
                    find_best(10, here)
                    find_best(11, here)
                if real(behind2):
                    route_best(1, behind2)
                if real(here):
                    find_best(12, here)
                    find_best(13, here)
                    find_best(14, here)
                    find_best(15, here)
                if real(behind2):
                    route_rest(1, behind2)
                if real(here):
                    find_best(16, here)
                    find_best(17, here)
                    find_best(18, here)
                    find_best(19, here)
                    find_best(20, here)
                    find_best(21, here)
                    find_best(22, here)
                if real(behind1):
                    weight_sums(behind1)
                if real(here):
                    find_best(23, here)
                if real(behind1):
                    context(behind1)
                if real(ahead1):
                    add_to_x(ahead1, y0_mm, pB[:, 128:256], x_moe0)
                if real(behind2):
                    keep_within(behind2)
                if real(ahead1):
                    stats(2, ahead1)
                if real(ahead2):
                    moments(0, ahead2)
                if real(ahead1):
                    moments(2, ahead1)
                if real(here):
                    find_best(24, here)
                    find_best(25, here)
                if real(behind2):
                    kept_rec(behind2)
                if real(ahead2):
                    stats(0, ahead2)
                if real(here):
                    find_best(26, here)
                    find_best(27, here)
                if real(behind1):
                    add_to_x(behind1, o1_mm, pD[:, 128:256], x_attn1)
                if real(here):
                    find_best(28, here)
                if real(behind2):
                    moe1_sum(0, behind2)
                if real(behind1):
                    stats(3, behind1)
                if real(here):
                    find_best(29, here)
                if real(behind1):
                    moments(3, behind1)
                if real(behind2):
                    moe1_sum(1, behind2)
                if real(here):
                    find_best(30, here)
                    find_best(31, here)
                if real(behind2):
                    moe1_last(behind2)

            iterations(dve, start, body, finish)

        @block.scalar
        def _(act):
            act.wait_ge(kv_mm, 1)
            for b in range(B):
                part = slice(b * QK, (b + 1) * QK)
                nc.scalar.activation(k0[part], R0[part, 0:KEYS], ACT.Identity,
                                     bias=e("bk0")[part]).then_inc(kv_act, 1)
            nc.scalar.activation(qsel_bias[:], e("sel")[0:2 * QK], ACT.Identity,
                                 scale=e("bq0")[0:2 * QK]).then_inc(kv_act, 1)

            def keys1():
                act.wait_ge(kv_mm, 2)
                nc.scalar.activation(k1[:].rearrange("p b k -> p (b k)"), W[0][:, 0:B * KEYS], ACT.Identity,
                                     bias=l("bk1")).then_inc(kv_act, 1)

            def xT_copy(k, t):
                act.wait_ge(xT_mm[k], t + 1)
                nc.scalar.activation(xT[k][:], xT_ps[k], ACT.Identity).then_inc(xT_in[k], 1)

            def attn0_q(t):
                if isinstance(t, int):
                    act.wait_ge(kv_act, 3)
                pass_when(act, q0_mm, t + 1)
                nc.scalar.activation(q0[:], pA[0:2 * QK, 128:256], ACT.Identity, scale=e("sel")[0:2 * QK, t:t + 1]
                                     if isinstance(t, int) else e("sel")[0:2 * QK, bass.ds(t, 1)],
                                     bias=qsel_bias[:, t:t + 1] if isinstance(t, int) else qsel_bias[:, bass.ds(t, 1)]
                                     ).then_inc(q0_act, 1)

            def attn0_tanh(t):
                act.wait_ge(z0_mm, t + 1)
                nc.scalar.activation(th0[:], pA[0:KEYS, 256:384], ACT.Tanh, scale=0.5 * QK ** -0.5).then_inc(tanh0, 1)

            def route_exp(k, t):
                act.wait_ge(rt_neg[k], t + 1)
                act.wait_ge(rt_rest[k], t + 1)
                nc.scalar.activation(gexp[k][:], logits[k], ACT.Exp, bias=gneg[k][:],
                                     accum_out=gsum[k][:]).then_inc(rt_exp[k], 1)

            def expert_act(j, t):
                act.wait_ge(h1_mm, 3 * t + j + 1)
                if j == 2 and real(t - 3):
                    act.wait_ge(hid_mm, t - 2)
                if j < 2:
                    nc.scalar.activation(act0[:, 4 * j:4 * j + 4, :].rearrange("p e i -> p (e i)"), R0[:],
                                         ACT.Silu).then_inc(h1_act, 1)
                else:
                    nc.scalar.activation(act0[:, E, :], R0[:, 0:INTER], ACT.Silu).then_inc(h1_act, 1)
                    nc.scalar.activation(lin0[:, E, :], R0[:, INTER:2 * INTER], ACT.Identity).then_inc(h3_act, 1)

            def expert_lin(j, t):
                act.wait_ge(c0_set, t + 1)
                act.wait_ge(h3_mm, 2 * t + j + 1)
                for n in range(4):
                    last = nc.scalar.activation(lin0[:, 4 * j + n, :], R1[:, n * INTER:(n + 1) * INTER], ACT.Identity,
                                                scale=c0[:, 4 * j + n:4 * j + n + 1])
                last.then_inc(h3_act, 1)

            def hidden_act(t):
                act.wait_ge(hid_mm, t + 1)
                nc.scalar.activation(hid[:], R0[:, 256:512], ACT.Silu).then_inc(hid_act, 1)

            def c0T_copy(t):
                act.wait_ge(c0T_mm, t + 1)
                nc.scalar.activation(c0T[:], c0T_ps, ACT.Identity).then_inc(c0T_act, 1)

            def gT_copy(j, t):
                act.wait_ge(g0T_mm, 3 * t + j + 1)
                if j == 2 and real(t - 3):
                    act.wait_ge(hidT_mm, t - 2)
                n = 4 if j < 2 else 1
                nc.scalar.activation(g0T[:, 4 * j:4 * j + n, :].rearrange("p e t -> p (e t)"),
                                     (R1, R0, R1)[j][:, 0:n * 128], ACT.Identity).then_inc(g0T_act, 1)

            def hidT_copy(t):
                act.wait_ge(hidT_mm, t + 1)
                nc.scalar.activation(hidT[:].rearrange("p k t -> p (k t)"), R1[:, 256:512],
                                     ACT.Identity).then_inc(hidT_act, 1)

            def y1_copy(n, t):
                act.wait_ge(c1_set, t + 1)
                act.wait_ge(y1_mm, 2 * t + n + 1)
                if not (isinstance(t, int) and t == 0):
                    act.wait_ge(y1_s4, t)
                for e in range(4):
                    last = nc.scalar.activation(y1[:, (4 * n + e) * D:(4 * n + e + 1) * D],
                                                (R0, R1)[n][:, e * D:(e + 1) * D], ACT.Identity,
                                                scale=c1[:, 4 * n + e:4 * n + e + 1])
                last.then_inc(y1_act, 1)

            def q1_copy(t):
                act.wait_ge(q1_mm, t + 1)
                nc.scalar.activation(qT1[:], pB[:, 384:512], ACT.Identity, bias=l("bq1")).then_inc(q1_act, 1)

            def scores_copy(g, t):
                act.wait_ge(s1_mm, GROUPS * t + g + 1)
                if not (isinstance(t, int) and t == 0):
                    act.wait_ge(exps, GROUPS * (t - 1) + g + 1)
                nc.scalar.activation(sw[g][:, 0, :], (R0, R1)[g % 2][:, 0:GK], ACT.Identity,
                                     scale=HD ** -0.5).then_inc(s1_act, 1)

            def weights_exp(g, t):
                act.wait_ge(less_max, GROUPS * t + g + 1)
                n = GROUPS * t + g
                if not (isinstance(t, int) and n < 2):
                    act.wait_ge(weights_set, n - 1)
                for h in range(HG):
                    cols = slice(h * KEYS, (h + 1) * KEYS)
                    last = nc.scalar.activation(ex[g % 2][:, :, cols], sw[g][:, :, cols], ACT.Exp,
                                                bias=peak[:, g * HG + h:g * HG + h + 1])
                last.then_inc(exps, 1)

            def pT_copy(g, t):
                n = GROUPS * t + g
                act.wait_ge(pT_mm, n + 1)
                if not (isinstance(t, int) and n < 2):
                    act.wait_ge(pv_mm, n - 1)
                nc.scalar.activation(pT[g % 2][:], W[g % 2][0:KEYS, :], ACT.Identity).then_inc(pT_act, 1)

            def cxT_copy(t):
                act.wait_ge(cxT_mm, t + 1)
                nc.scalar.activation(cxT[:], pD[:, 0:128], ACT.Identity).then_inc(cxT_act, 1)

            def start(i):
                ahead2, ahead1, here, behind1, behind2 = i + 2, i + 1, i, i - 1, i - 2
                if real(ahead1):
                    expert_lin(0, ahead1)
                if real(behind1):
                    pT_copy(2, behind1)
                if i == -1:
                    keys1()
                if real(ahead1):
                    expert_act(1, ahead1)
                    expert_lin(1, ahead1)
                if real(behind1):
                    pT_copy(3, behind1)
                if real(behind2):
                    hidden_act(behind2)
                if real(ahead2):
                    xT_copy(0, ahead2)
                if real(ahead1):
                    c0T_copy(ahead1)
                    expert_act(2, ahead1)
                if real(behind2):
                    route_exp(1, behind2)
                if real(ahead1):
                    gT_copy(0, ahead1)
                if real(here):
                    weights_exp(0, here)
                if real(ahead1):
                    gT_copy(1, ahead1)
                if real(ahead2):
                    attn0_q(ahead2)
                if real(ahead1):
                    gT_copy(2, ahead1)
                if real(behind2):
                    hidT_copy(behind2)
                if real(here):
                    weights_exp(1, here)
                if real(ahead2):
                    attn0_tanh(ahead2)
                if real(behind1):
                    cxT_copy(behind1)
                if real(here):
                    weights_exp(2, here)
                if real(behind2):
                    y1_copy(0, behind2)
                if real(here):
                    pT_copy(0, here)
                if real(ahead1):
                    xT_copy(2, ahead1)
                if real(behind2):
                    y1_copy(1, behind2)
                if real(ahead1):
                    q1_copy(ahead1)
                if real(here):
                    pT_copy(1, here)
                if real(ahead1):
                    scores_copy(0, ahead1)
                    scores_copy(1, ahead1)
                if real(ahead2):
                    xT_copy(1, ahead2)
                if real(ahead1):
                    scores_copy(2, ahead1)
                if real(here):
                    weights_exp(3, here)
                if real(ahead1):
                    scores_copy(3, ahead1)
                if real(behind1):
                    xT_copy(3, behind1)
                if real(ahead2):
                    route_exp(0, ahead2)
                    expert_act(0, ahead2)

            def body(i):
                ahead2, ahead1, here, behind1, behind2 = i + 2, i + 1, i, i - 1, i - 2
                expert_lin(0, ahead1)
                expert_act(1, ahead1)
                pT_copy(2, behind1)
                expert_lin(1, ahead1)
                hidden_act(behind2)
                expert_act(2, ahead1)
                xT_copy(0, ahead2)
                c0T_copy(ahead1)
                route_exp(1, behind2)
                attn0_q(ahead2)
                gT_copy(0, ahead1)
                pT_copy(3, behind1)
                gT_copy(1, ahead1)
                hidT_copy(behind2)
                gT_copy(2, ahead1)
                attn0_tanh(ahead2)
                weights_exp(0, here)
                weights_exp(1, here)
                weights_exp(2, here)
                xT_copy(2, ahead1)
                cxT_copy(behind1)
                y1_copy(0, behind2)
                pT_copy(0, here)
                q1_copy(ahead1)
                y1_copy(1, behind2)
                scores_copy(0, ahead1)
                xT_copy(1, ahead2)
                weights_exp(3, here)
                scores_copy(1, ahead1)
                scores_copy(2, ahead1)
                pT_copy(1, here)
                xT_copy(3, behind1)
                scores_copy(3, ahead1)
                route_exp(0, ahead2)
                expert_act(0, ahead2)

            def finish(i):
                ahead2, ahead1, here, behind1, behind2 = i + 2, i + 1, i, i - 1, i - 2
                if real(ahead2):
                    attn0_q(ahead2)
                if real(ahead1):
                    expert_lin(0, ahead1)
                    expert_act(1, ahead1)
                if real(ahead2):
                    route_exp(0, ahead2)
                if real(behind1):
                    pT_copy(2, behind1)
                if real(ahead1):
                    expert_lin(1, ahead1)
                    expert_act(2, ahead1)
                if real(behind2):
                    hidden_act(behind2)
                if real(behind1):
                    pT_copy(3, behind1)
                if real(ahead1):
                    gT_copy(0, ahead1)
                if real(behind2):
                    if behind2 < TILES - 1:
                        route_exp(1, behind2)
                if real(ahead1):
                    c0T_copy(ahead1)
                    gT_copy(1, ahead1)
                    gT_copy(2, ahead1)
                if real(here):
                    weights_exp(0, here)
                if real(behind2):
                    hidT_copy(behind2)
                    if behind2 == TILES - 1:
                        route_exp(1, behind2)
                if real(here):
                    weights_exp(1, here)
                    weights_exp(2, here)
                if real(behind1):
                    cxT_copy(behind1)
                if real(ahead1):
                    xT_copy(2, ahead1)
                if real(here):
                    pT_copy(0, here)
                if real(ahead2):
                    xT_copy(0, ahead2)
                if real(behind2):
                    y1_copy(0, behind2)
                if real(ahead2):
                    attn0_tanh(ahead2)
                    xT_copy(1, ahead2)
                if real(ahead1):
                    q1_copy(ahead1)
                    scores_copy(0, ahead1)
                if real(behind2):
                    y1_copy(1, behind2)
                if real(ahead2):
                    expert_act(0, ahead2)
                if real(here):
                    pT_copy(1, here)
                if real(ahead1):
                    scores_copy(1, ahead1)
                    scores_copy(2, ahead1)
                if real(here):
                    weights_exp(3, here)
                if real(behind1):
                    xT_copy(3, behind1)
                if real(ahead1):
                    scores_copy(3, ahead1)

            iterations(act, start, body, finish)

        @block.gpsimd
        def _(pool):
            def spread_keys():
                pool.wait_ge(kv_act, 4)
                for b in range(B):
                    nc.gpsimd.tensor_tensor(kbd[:, b], k1[:, b, :].unsqueeze(1).to_broadcast([D, HEADS, KEYS]),
                                            l("headmask").unsqueeze(2).to_broadcast([D, HEADS, KEYS]),
                                            ALU.mult).then_inc(kv_pool, 1)

            def rstd(k, t):
                pool.wait_ge(ln_mv[k], t + 1)
                nc.gpsimd.tensor_tensor(lnve[k][:], lnmv[k][:, 1:2], eps_t[:], ALU.add).then_inc(ln_ve[k], 1)
                pool.wait_ge(ln_ve[k], t + 1)
                nc.gpsimd.tensor_tensor(lnrs[k][:], lnve[k][:], half_t[:], ALU.pow).then_inc(ln_rstd[k], 1)

            def centre(k, t):
                pass_when(pool, ln_mv[k], t + 1)
                nc.gpsimd.tensor_tensor(xc[k][:], x[:, t, :], lnmv[k][:, 0:1].to_broadcast([P, D]),
                                        ALU.subtract).then_inc(ln_mid[k], 1)

            def normalise(k, t):
                pool.wait_ge(ln_mid[k], t + 1)
                pool.wait_ge(ln_rstd[k], t + 1)
                nc.gpsimd.tensor_tensor(xn[k][:], xc[k][:], lnrs[k][:].to_broadcast([P, D]),
                                        ALU.mult).then_inc(ln_done[k], 1)

            def attn0_sigmoid(t):
                pass_when(pool, tanh0, t + 1)
                nc.gpsimd.tensor_scalar(sg0[:], th0[:], 0.5, 0.5, ALU.mult, ALU.add).then_inc(sigm0, 1)

            def route_pad(k, t):
                pass_when(pool, rt_max[k], t + 1)
                nc.gpsimd.memset(gmax[k][:, 2:8], TAKEN).then_inc(rt_pad[k], 1)
                nc.gpsimd.tensor_scalar(gneg[k][:], gmax[k][:, 0:1], -1.0, None, ALU.mult).then_inc(rt_neg[k], 1)

            def route_mask(k, t):
                pass_when(pool, rt_rest[k], t + 1)
                nc.gpsimd.tensor_scalar(gmask[k][:], grest[k][:], TAKEN, None, ALU.is_equal).then_inc(rt_mask[k], 1)

            def route_two(k, t):
                pool.wait_ge(rt_mask[k], t + 1)
                pool.wait_ge(rt_exp[k], t + 1)
                nc.gpsimd.tensor_tensor(gtwo[k][:], gexp[k][:], gmask[k][:], ALU.mult).then_inc(rt_two[k], 1)

            def kept_sum(t):
                pass_when(pool, tg_set, t + 1)
                nc.gpsimd.tensor_scalar(tge[:], gsum[1][:], 1e-6, tgs[:], ALU.mult, ALU.add).then_inc(tge_set, 1)

            def combine1(t):
                if not (isinstance(t, int) and t == 0):
                    pool.wait_ge(y1_act, 2 * t)
                pool.wait_ge(tgr_set, t + 1)
                nc.gpsimd.tensor_tensor(c1[:], tg[:], tgr[:].to_broadcast([P, E]), ALU.mult).then_inc(c1_set, 1)

            def combine0(t):
                pool.wait_ge(rt_two[0], t + 1)
                pool.wait_ge(rt_rec, t + 1)
                nc.gpsimd.tensor_tensor(c0[:, 0:E], gtwo[0][:], grec0[:].to_broadcast([P, E]),
                                        ALU.mult).then_inc(c0_set, 1)

            def gate_experts(j, t):
                if isinstance(t, int) and t == 0:
                    return
                pool.wait_ge(h1_act, 3 * t + j + 1)
                pool.wait_ge(h3_act, 3 * t + j + 1)
                part = slice(4 * j, min(4 * j + 4, E + 1))
                nc.gpsimd.tensor_tensor(g0[:, part], lin0[:, part], act0[:, part], ALU.mult).then_inc(g0_set, 1)

            def add_bo(t):
                pass_when(pool, ln_done[2], t + 1)
                nc.gpsimd.tensor_tensor(x[:, t, :], x[:, t, :], bo, ALU.add).then_inc(x_bo, 1)

            def less_maximum(g, t):
                pass_when(pool, best_found, HEADS * t + HG * (g + 1))
                nc.gpsimd.tensor_scalar(peak[:, g * HG:(g + 1) * HG], top1[:, g * HG:(g + 1) * HG, 0], -1.0, None,
                                        ALU.mult).then_inc(less_max, 1)

            def keep_best(g, t):
                n = GROUPS * t + g
                pool.wait_ge(exps, n + 1)
                if not (isinstance(t, int) and n < 2):
                    pool.wait_ge(pT_mm, n - 1)
                nc.gpsimd.tensor_tensor(pw[g % 2][:], ex[g % 2][:, 0], ex[g % 2][:, 1], ALU.subtract).then_inc(weights_set, 1)

            def count_kept(t):
                pool.wait_ge(cnt_mm, t + 1)
                nc.gpsimd.tensor_tensor(kept_before[:], kept_before[:], gmask[1][:], ALU.add).then_inc(kept_add, 1)

            def moe1_add(t):
                if isinstance(t, int) and t == TILES - 1:
                    return
                pool.wait_ge(y1_act, 2 * t + 2)
                nc.gpsimd.tensor_tensor(s4[:], y1[:, 0:4 * D], y1[:, 4 * D:], ALU.add).then_inc(y1_s4, 1)

            def moe1_end(t):
                if isinstance(t, int) and t == TILES - 1:
                    return
                pool.wait_ge(y1_s4, t + 1)
                nc.gpsimd.tensor_tensor(s2[:], s4[:, 0:2 * D], s4[:, 2 * D:], ALU.add).then_inc(y1_s2, 1)
                pool.wait_ge(y1_s2, t + 1)
                nc.gpsimd.tensor_tensor(s1[:], s2[:, 0:D], s2[:, D:], ALU.add).then_inc(y1_s1, 1)
                pass_when(pool, y1_s1, t + 1)
                pass_when(pool, stored, 16 * (t + 1))
                nc.gpsimd.tensor_tensor(xo[:], s1[:], x[:, t, :], ALU.add).then_inc(xo_set, 1)

            nc.gpsimd.memset(kept_before[:], 0.0).then_inc(kept_add, 1)
            nc.gpsimd.memset(xo[:], 0.0).then_inc(stored, 16)

            def start(i):
                ahead2, ahead1, here, behind1, behind2 = i + 2, i + 1, i, i - 1, i - 2
                if i == -2:
                    pool.wait_ge(consts_set, 5)
                if real(ahead2):
                    centre(0, ahead2)
                    rstd(0, ahead2)
                if real(ahead1):
                    gate_experts(0, ahead1)
                if real(ahead2):
                    normalise(0, ahead2)
                if real(here):
                    less_maximum(0, here)
                if real(behind2):
                    route_mask(1, behind2)
                if real(ahead1):
                    gate_experts(1, ahead1)
                if i == -1:
                    spread_keys()
                if real(ahead1):
                    gate_experts(2, ahead1)
                if real(behind2):
                    route_two(1, behind2)
                if real(here):
                    add_bo(here)
                if real(behind2):
                    kept_sum(behind2)
                if real(here):
                    keep_best(0, here)
                    less_maximum(1, here)
                    less_maximum(2, here)
                if real(ahead2):
                    attn0_sigmoid(ahead2)
                if real(ahead1):
                    centre(2, ahead1)
                if real(behind2):
                    combine1(behind2)
                if real(ahead1):
                    rstd(2, ahead1)
                    normalise(2, ahead1)
                if real(here):
                    keep_best(1, here)
                    keep_best(2, here)
                if real(ahead2):
                    rstd(1, ahead2)
                    centre(1, ahead2)
                    normalise(1, ahead2)
                if real(here):
                    less_maximum(3, here)
                if real(behind1):
                    rstd(3, behind1)
                    centre(3, behind1)
                    normalise(3, behind1)
                if real(ahead2):
                    route_pad(0, ahead2)
                if real(behind2):
                    moe1_add(behind2)
                if real(ahead2):
                    route_mask(0, ahead2)
                    route_two(0, ahead2)
                    combine0(ahead2)
                if real(behind2):
                    count_kept(behind2)
                    moe1_end(behind2)
                if real(behind1):
                    route_pad(1, behind1)
                if real(here):
                    keep_best(3, here)

            def body(i):
                ahead2, ahead1, here, behind1, behind2 = i + 2, i + 1, i, i - 1, i - 2
                centre(0, ahead2)
                rstd(0, ahead2)
                normalise(0, ahead2)
                gate_experts(0, ahead1)
                gate_experts(1, ahead1)
                less_maximum(0, here)
                route_mask(1, behind2)
                route_two(1, behind2)
                gate_experts(2, ahead1)
                kept_sum(behind2)
                less_maximum(1, here)
                attn0_sigmoid(ahead2)
                less_maximum(2, here)
                keep_best(0, here)
                centre(2, ahead1)
                rstd(2, ahead1)
                combine1(behind2)
                normalise(2, ahead1)
                rstd(1, ahead2)
                keep_best(1, here)
                centre(1, ahead2)
                add_bo(here)
                normalise(1, ahead2)
                keep_best(2, here)
                less_maximum(3, here)
                count_kept(behind2)
                rstd(3, behind1)
                centre(3, behind1)
                normalise(3, behind1)
                route_pad(0, ahead2)
                moe1_add(behind2)
                route_mask(0, ahead2)
                route_two(0, ahead2)
                combine0(ahead2)
                moe1_end(behind2)
                keep_best(3, here)
                route_pad(1, behind1)

            def finish(i):
                ahead2, ahead1, here, behind1, behind2 = i + 2, i + 1, i, i - 1, i - 2
                if real(ahead2):
                    centre(1, ahead2)
                if real(ahead1):
                    gate_experts(0, ahead1)
                if real(here):
                    less_maximum(0, here)
                if real(ahead1):
                    gate_experts(1, ahead1)
                if real(ahead2):
                    route_mask(0, ahead2)
                if real(here):
                    less_maximum(1, here)
                if real(behind2):
                    route_mask(1, behind2)
                if real(ahead1):
                    gate_experts(2, ahead1)
                if real(here):
                    add_bo(here)
                if real(behind2):
                    route_two(1, behind2)
                if real(here):
                    keep_best(0, here)
                if real(ahead2):
                    combine0(ahead2)
                if real(here):
                    less_maximum(2, here)
                if real(behind2):
                    count_kept(behind2)
                    kept_sum(behind2)
                if real(ahead1):
                    centre(2, ahead1)
                    rstd(2, ahead1)
                    normalise(2, ahead1)
                if real(here):
                    keep_best(1, here)
                if real(ahead2):
                    rstd(0, ahead2)
                if real(behind2):
                    combine1(behind2)
                if real(here):
                    keep_best(2, here)
                if real(behind1):
                    rstd(3, behind1)
                if real(ahead2):
                    normalise(1, ahead2)
                    route_two(0, ahead2)
                if real(behind1):
                    centre(3, behind1)
                if real(ahead2):
                    centre(0, ahead2)
                if real(here):
                    less_maximum(3, here)
                if real(behind1):
                    normalise(3, behind1)
                if real(ahead2):
                    rstd(1, ahead2)
                if real(here):
                    keep_best(3, here)
                if real(ahead2):
                    normalise(0, ahead2)
                    route_pad(0, ahead2)
                    attn0_sigmoid(ahead2)
                if real(behind2):
                    moe1_add(behind2)
                if real(behind1):
                    route_pad(1, behind1)
                if real(behind2):
                    moe1_end(behind2)

            iterations(pool, start, body, finish)


def kernel(**inputs):
    import numpy as np
    import concourse.bacc as bacc
    from concourse.bass_utils import run_bass_kernel_spmd

    a = {k: np.asarray(v) for k, v in inputs.items()}
    f = np.float32

    def pad(v):
        v = v.reshape(-1, 1) if v.ndim == 1 else v
        return np.concatenate([v, np.zeros((128 - v.shape[0], v.shape[1]), f)]) if v.shape[0] < 128 else v

    batch_rows = np.repeat(np.eye(B, dtype=f), QK, axis=0)
    early = {
        "ident": np.eye(128, dtype=f),
        "ctxT": a["ctx_1024"].reshape(B * KEYS, D).T,
        "wk0": a["L0_xattn_Wk"].T,
        "wq0": np.concatenate([a["L0_xattn_Wq"].T] * 2, axis=1),
        "wv0": a["L0_xattn_Wv"].T,
        "bq0": np.concatenate([a["L0_xattn_bq"]] * 2),
        "bk0": np.concatenate([a["L0_xattn_bk"]] * 2),
        "sel": np.repeat(batch_rows, PER_BATCH, axis=1),
        "iota": np.tile(np.arange(E, dtype=f), (128, 1)),
        "gate": a["L0_ffn_gate_w"].T,
    }
    late = {
        "wq1": a["L1_xattn_Wq"].T,
        "wk1": a["L1_xattn_Wk"].T,
        "wv1": a["L1_xattn_Wv"].T,
        "wo1": a["L1_xattn_Wo"].T,
        "router": a["L1_ffn_w_router"].T,
        "wg": a["L1_ffn_w_gate"].T,
        "triu": np.triu(np.ones((128, 128), f)),
        "ones": np.ones((128, 128), f),
        "headmask": np.repeat(np.eye(HEADS, dtype=f), HD, axis=0),
        "bq1": a["L1_xattn_bq"],
        "bk1": a["L1_xattn_bk"],
        "bias": np.concatenate([a["L0_ffn_b1"].reshape(-1), a["L0_ffn_b3"].reshape(-1), a["L0_ffn_sb1"],
                                a["L0_ffn_sb3"]]).reshape(128, 18),
    }
    arrays = {
        "early": np.concatenate([pad(early[n]) for n, _ in EARLY], axis=1),
        "late": np.concatenate([pad(late[n]) for n, _ in LATE], axis=1),
        "x": a["x"].reshape(TILES, P, D),
        "rows": np.concatenate([a["L0_xattn_bv"], a["L1_xattn_bv"], a["L1_xattn_bo"]]),
        "w1": a["L0_ffn_w1"].transpose(1, 0, 2).reshape(D, E * INTER),
        "w3": a["L0_ffn_w3"].transpose(1, 0, 2).reshape(D, E * INTER),
        "w2": a["L0_ffn_w2"].transpose(1, 0, 2).reshape(INTER, E * D),
        "sw13": np.concatenate([a["L0_ffn_sw1"], a["L0_ffn_sw3"]], axis=1),
        "sw2": a["L0_ffn_sw2"],
        "b2": np.concatenate([a["L0_ffn_b2"], a["L0_ffn_sb2"].reshape(1, D)]),
        "wd": a["L1_ffn_w_down"].transpose(2, 0, 1).reshape(2, 128, E * D).transpose(1, 0, 2),
    }
    nc = bacc.Bacc("TRN2", target_bir_lowering=False, num_devices=1)
    feed, args = {}, []
    for name, v in arrays.items():
        v = np.ascontiguousarray(v)
        feed[name + "_dram"] = v
        args.append(nc.dram_tensor(name + "_dram", v.shape, mybir.dt.from_np(v.dtype), kind="ExternalInput").ap())
    out = nc.dram_tensor("out_dram", (TILES, P, D), F32, kind="ExternalOutput").ap()
    build(nc, *args, out)
    r = run_bass_kernel_spmd(nc, [feed], core_ids=[0])
    return r.results[0]["out_dram"].reshape(B, S, D)
```
